# Optimizing a Trainium2 kernel written in Bass

```python
import numpy as np
import jax
import jax.numpy as jnp

def _softmax(x, axis=-1):
    return jax.nn.softmax(x, axis=axis)

def _gelu(x):
    return jax.nn.gelu(x, approximate=True)

def _silu(x):
    return jax.nn.silu(x)

def _sigmoid(x):
    return jax.nn.sigmoid(x)

def _layernorm(x, axis=-1, eps=1e-05):
    m = jnp.mean(x, axis=axis, keepdims=True)
    v = jnp.var(x, axis=axis, keepdims=True)
    return (x - m) / jnp.sqrt(v + eps)

def _scatter_add(tgt, idx, src, axis=0):
    return tgt.at[idx].add(src)

def _segment_sum(src, seg, n):
    return jax.ops.segment_sum(src, seg, n)
kernel_name = 'mk_adaln_ffn_d1_seqx_r4_1817b6'

def setup_inputs(seed: int=0):
    np.random.seed(seed)
    _w = jnp.asarray

    def _rec_inputs():
        import jax
        import jax.numpy as jnp
        _rk = jax.random.key(seed)
        x = -0.000125 + 0.9999 * jax.random.normal(jax.random.fold_in(_rk, 1), (8, 256, 1024), jnp.float32)
        _lenS = 256 - jax.random.randint(jax.random.fold_in(_rk, 7), (8,), 0, max(1, 256 // 4) + 1, jnp.int32)
        _lenS2 = 256 - jax.random.randint(jax.random.fold_in(_rk, 8), (8,), 0, max(1, 256 // 4) + 1, jnp.int32)
        itok_B_0_7 = jax.random.randint(jax.random.fold_in(_rk, 11), (8,), 0, 8, jnp.int32)
        return (x, itok_B_0_7)
    x, itok_B_0_7 = _rec_inputs()

    def _L0_cond_setup():
        import jax, jax.numpy as jnp
        import numpy as np
        TOP_K = 2
        LANG_BIAS = 5.0
        SCALING = 32.0 / 16.0
        LANGUAGE_PAD_ID = -1
        key = jax.random.key(seed)
        ks = jax.random.split(key, 6)
        B, T, D, O, E, R = (4, 512, 1024, 1024, 8, 16)
        x = jax.random.normal(ks[0], (B, T, D), dtype=jnp.float32)
        language_ids = jax.random.randint(ks[1], (B,), 0, E).astype(jnp.int64)
        W = jax.random.normal(ks[2], (O, D), dtype=jnp.float32) * (1.0 / np.sqrt(D))
        Wr = jax.random.normal(ks[3], (E, D), dtype=jnp.float32) * (1.0 / np.sqrt(D))
        A = jax.random.normal(ks[4], (E, R, D), dtype=jnp.float32) * (1.0 / np.sqrt(D))
        Bm = jax.random.normal(ks[5], (O, R), dtype=jnp.float32) * 0.0
        Bm = jnp.broadcast_to(Bm, (E, O, R)) + jax.random.normal(ks[5], (E, O, R), dtype=jnp.float32) * 0.02
        return {'x': x, 'language_ids': language_ids, 'W': W, 'Wr': Wr, 'A': A, 'B': Bm}
    _L0_cond_all = _L0_cond_setup()
    _L0_cond_in = {k: v for k, v in _L0_cond_all.items() if k in ('W', 'Wr', 'A', 'B')}
    del _L0_cond_all

    def _L0_ffn_setup():
        import jax, jax.numpy as jnp
        import numpy as np
        IN_F = 1024
        OUT_F = 1024
        N_CLUSTERS = 64
        THRESHOLD = 0.01
        TEMPERATURE = 0.1
        BATCH, SEQ = (4, 512)
        key = jax.random.key(seed)
        k1, k2, k3, k4, k5 = jax.random.split(key, 5)
        s = 1.0 / np.sqrt(IN_F)
        return {'input': jax.random.normal(k1, (BATCH, SEQ, IN_F), dtype=jnp.float32), 'weight': jax.random.normal(k2, (OUT_F, IN_F), dtype=jnp.float32) * s, 'bias': jax.random.uniform(k3, (OUT_F,), dtype=jnp.float32, minval=-s, maxval=s), 'centroids': jax.random.normal(k4, (N_CLUSTERS, IN_F), dtype=jnp.float32) * s, 'assignments': jax.random.randint(k5, (OUT_F,), 0, N_CLUSTERS, dtype=jnp.int32)}
    _L0_ffn_all = _L0_ffn_setup()
    _L0_ffn_in = {k: v for k, v in _L0_ffn_all.items() if k in ('weight', 'bias', 'centroids', 'assignments')}
    del _L0_ffn_all
    return {'x': x, 'itok_B_0_7': itok_B_0_7, 'L0_cond_W': _L0_cond_in['W'], 'L0_cond_Wr': _L0_cond_in['Wr'], 'L0_cond_A': _L0_cond_in['A'], 'L0_cond_B': _L0_cond_in['B'], 'L0_ffn_weight': _L0_ffn_in['weight'], 'L0_ffn_bias': _L0_ffn_in['bias'], 'L0_ffn_centroids': _L0_ffn_in['centroids'], 'L0_ffn_assignments': _L0_ffn_in['assignments']}

def reference(x, itok_B_0_7, L0_cond_W, L0_cond_Wr, L0_cond_A, L0_cond_B, L0_ffn_weight, L0_ffn_bias, L0_ffn_centroids, L0_ffn_assignments):
    import jax
    import jax.numpy as jnp

    def _L0_cond_ref(x, language_ids, W, Wr, A, B):
        import jax, jax.numpy as jnp
        import numpy as np
        TOP_K = 2
        LANG_BIAS = 5.0
        SCALING = 32.0 / 16.0
        LANGUAGE_PAD_ID = -1
        base = jnp.einsum('btd,od->bto', x, W)
        E = Wr.shape[0]
        logits = jnp.einsum('btd,ed->bte', x.astype(jnp.float32), Wr.astype(jnp.float32))
        expert_targets = language_ids
        valid = expert_targets >= 0
        tgt = jnp.where(valid, expert_targets, 0)
        bias = jax.nn.one_hot(tgt, E, dtype=logits.dtype) * LANG_BIAS
        bias = jnp.where(valid[:, None], bias, 0.0)
        logits = logits + bias[:, None, :]
        topw, topi = jax.lax.top_k(logits, TOP_K)
        weights = jax.nn.softmax(topw, axis=-1)
        gates = jnp.sum(jax.nn.one_hot(topi, E, dtype=weights.dtype) * weights[..., None], axis=-2)
        gates = gates.astype(x.dtype)
        h = jnp.einsum('btd,erd->bter', x, A)
        lora_out = jnp.einsum('bter,bte,eor->bto', h, gates, B)
        return base + SCALING * lora_out

    def _L0_ffn_ref(input, weight, bias, centroids, assignments):
        import jax, jax.numpy as jnp
        import numpy as np
        IN_F = 1024
        OUT_F = 1024
        N_CLUSTERS = 64
        THRESHOLD = 0.01
        TEMPERATURE = 0.1
        BATCH, SEQ = (4, 512)
        shape = input.shape
        x = input.reshape(-1, shape[-1])
        dots = jax.nn.softmax(x @ centroids.T / TEMPERATURE, axis=-1)
        hits = dots > THRESHOLD
        query_sel = jnp.any(hits, axis=1)
        cluster_sel = jnp.any(hits, axis=0)
        row_sel = cluster_sel[assignments]
        dense = x @ weight.T + bias
        out = jnp.where(query_sel[:, None] & row_sel[None, :], dense, jnp.zeros((), dense.dtype))
        return out.reshape(*shape[:-1], -1)
    x = x + _L0_ffn_ref(_L0_cond_ref(x, itok_B_0_7, L0_cond_W, L0_cond_Wr, L0_cond_A, L0_cond_B), L0_ffn_weight, L0_ffn_bias, L0_ffn_centroids, L0_ffn_assignments)
    return x

_drawn_inputs = setup_inputs


def setup_inputs(seed=0):
    import zlib

    import numpy as np

    out = dict(_drawn_inputs(seed))
    spreads = {}
    factors = {'L0_cond_Wr': 4.992, 'L0_ffn_bias': 4.394}
    for name, (base, spread) in spreads.items():
        noise = np.random.default_rng([zlib.crc32(name.encode()), seed]).standard_normal(out[name].shape)
        drawn = base * np.exp(spread * noise) if base else spread * noise
        out[name] = jnp.asarray(drawn.astype(out[name].dtype))
    for name, factor in factors.items():
        out[name] = (out[name] * factor).astype(out[name].dtype)
    return out
```

```python
from contextlib import ExitStack

import concourse.bass as bass
from concourse import mybir

ALU = mybir.AluOpType
ACT = mybir.ActivationFunctionType
AX_X = mybir.AxisListType.X
F32 = mybir.dt.float32
F32R = mybir.dt.float32r
BF16 = mybir.dt.bfloat16
I32 = mybir.dt.int32
U32 = mybir.dt.uint32

P = 128
HALF = 512
LANG_BIAS = 5.0
SCALING = 2.0
THRESHOLD = 0.01
TEMPERATURE = 0.1



def adaln_ffn_kernel(nc, x, ids, W, Wr, A, B, V, bias, cent, assign, out):
    NB, S, D = x.shape
    O = W.shape[0]
    E, R, _ = A.shape
    C = cent.shape[0]
    FO = V.shape[0]
    ER = E * R
    T = NB * S
    NT = T // P
    NPAIR = NT // 2
    KD = D // P
    KO = O // P
    KG = KD + 1
    AW = ER + E
    AWG = AW + C
    F1 = HALF - C
    F2 = FO - F1
    CH = F2 // 2
    V1_TURNS, V2_TURNS = 4, KD - 2
    V1_ROWS, V2_ROWS = F1 // V1_TURNS, F2 // V2_TURNS
    TURN_V2 = V1_TURNS
    TURN_A = TURN_V2 + V2_TURNS
    TURN_PAIR = TURN_A + 1
    TURN_MAIN = TURN_PAIR + NT
    G_BASE = [(KG + 1) // 2, KG // 2]
    assert S == 2 * P and ER == P and KD == KO == NPAIR == 8 and FO == 2 * HALF and C < P and E <= 8

    x_t = x.rearrange("b s d -> (b s) d")
    out_t = out.rearrange("b s d -> (b s) d")
    W_t = W.rearrange("(p j) d -> p j d", j=KO)
    B_t = B.rearrange("e (p j) r -> p e (j r)", j=KO)

    def b_view(raw):
        return raw[:].rearrange("p (e a) b -> p e (a b)", e=E)

    def b_raw_view(raw):
        return raw[:].rearrange("p e (j r) -> p j e r", r=R)

    def b_split_view(split):
        return split[:].rearrange("p j (e r) -> p j e r", r=R)

    with ExitStack() as ctx:
        def sb(name, shape, dt, stack=ctx):
            return stack.enter_context(nc.sbuf_tensor(name, shape, dt))

        def sem(name):
            return ctx.enter_context(nc.semaphore(name))

        ident = sb("ident", [P, P], F32)
        aw_hi = sb("aw_hi", [P, KD, AWG], F32R)
        aw_lo = sb("aw_lo", [P, KD, AWG], F32R)
        gb_hi = sb("gb_hi", [P, C], F32R)
        gb_lo = sb("gb_lo", [P, C], F32R)
        onehot_a = sb("onehot_a", [C, FO], BF16)
        iota8 = sb("iota8", [P, E], F32)
        pidx = sb("pidx", [P, 1], F32)
        lang_bias = sb("lang_bias", [P, NB, E], F32)
        ones_b = sb("ones_b", [P, P], BF16)
        hit_sum = sb("hit_sum", [P, 2, C], F32)
        hit_b = sb("hit_b", [P, 2, C], BF16)
        csel = sb("csel", [C, P], BF16)
        qsel = sb("qsel", [P, NT], F32)
        rl = sb("rl", [P, 2, E], F32)
        m8 = sb("m8", [P, 2, 8], F32)
        idx8 = sb("idx8", [P, 2, 8], U32)
        diff = sb("diff", [P, 2], F32)
        e2 = sb("e2", [P, 2], F32)
        den = sb("den", [P, 2], F32)
        wts = sb("wts", [P, 2, 2], F32)
        pick = sb("pick", [P, 2, 2, E], F32)
        gates = sb("gates", [P, 2, E], F32)
        hg = sb("hg", [P, 2, ER], F32)
        mx = sb("mx", [P, 2], F32)
        negb = sb("negb", [P, 2], F32)
        ex = sb("ex", [P, 2, C], F32)
        esum = sb("esum", [P, 2], F32)
        rsum = sb("rsum", [P, 2], F32)
        hits = sb("hits", [P, 2, C], F32)

        with ExitStack() as early:
            vraw = [sb(f"vraw{b}", [P, O], F32, early) for b in range(2)]
            as_raw = sb("as_raw", [C, FO], I32, early)
            with ExitStack() as earliest:
                cent_raw = sb("cent_raw", [C, O], F32, earliest)
                vraw += [sb(f"vraw{b}", [P, O], F32, earliest) for b in (2, 3)]
            as_neg = sb("as_neg", [C, FO], F32, early)
            a_raw = sb("a_raw", [ER, D], F32, early)
            wr_raw = sb("wr_raw", [E, D], F32, early)
        xraw = [sb(f"xraw{b}", [P, D], F32) for b in range(2)]
        xt_hi = [sb("xt0_hi", [P, KD, P], F32R), None]
        xt_lo = [sb("xt0_lo", [P, KD, P], F32R), None]
        hgt_all = sb("hgt_all", [P, T], F32)
        ids_raw = sb("ids_raw", [P, NB], I32)

        g_hi = sb("g_hi", [P, KG, FO], F32R)
        g_lo = sb("g_lo", [P, KG, FO], F32R)

        vt2_hi = sb("vt2_hi", [P, KO, F2], F32R)
        vt2_lo = sb("vt2_lo", [P, KO, F2], F32R)
        wraw = [sb(f"wraw{b}", [P, KO, P], F32) for b in range(2)]
        w_hi = [sb(f"w{b}_hi", [P, KO, P], F32R) for b in range(2)]
        w_lo = [sb(f"w{b}_lo", [P, KO, P], F32R) for b in range(2)]
        with ExitStack() as first_sweep:
            vt1_hi = sb("vt1_hi", [P, KO, HALF], F32R, first_sweep)
            vt1_lo = sb("vt1_lo", [P, KO, HALF], F32R, first_sweep)
        xt_hi[1] = sb("xt1_hi", [P, KD, P], F32R)
        xt_lo[1] = sb("xt1_lo", [P, KD, P], F32R)
        hgt_hi = sb("hgt_hi", [P, 2 * P], F32R)
        hgt_lo = sb("hgt_lo", [P, 2 * P], F32R)
        hx_hi = [sb(f"hx{b}_hi", [P, P], F32R) for b in range(2)]
        hx_lo = [sb(f"hx{b}_lo", [P, P], F32R) for b in range(2)]
        bias_row = sb("bias_row", [P, FO], F32)
        mask_row = sb("mask_row", [P, FO], F32)
        dense = sb("dense", [P, FO], F32)
        xkeep = [sb(f"xkeep{b}", [P, FO], F32) for b in range(2)]

        ps_turn = ctx.enter_context(nc.psum_tensor("ps_turn", [P, 2, HALF], F32))
        ps_aw = ctx.enter_context(nc.psum_tensor("ps_aw", [P, 2, HALF], F32))
        ps_out = ctx.enter_context(nc.psum_tensor("ps_out", [P, 2, FO], F32))
        ps_g = [ps_out[:, 0, c * HALF:(c + 1) * HALF] for c in range(2)]
        ps_hgt = ps_out[:, 1, 0:2 * P]

        cent_landed = sem("cent_landed")
        small_landed = sem("small_landed")
        assign_landed = sem("assign_landed")
        bias_landed = sem("bias_landed")
        w_landed = [sem(f"w_landed{b}") for b in range(2)]
        v_landed = [sem(f"v_landed{b}") for b in range(4)]
        x_landed = [sem(f"x_landed{b}") for b in range(2)]
        out_stored = [sem(f"out_stored{b}") for b in range(2)]
        const_ready = sem("const_ready")
        setup_step = sem("setup_step")
        small_turned = sem("small_turned")
        small_hi = sem("small_hi")
        small_lo = sem("small_lo")
        turned = [sem(f"turned{h}") for h in range(2)]
        turn_hi = [sem(f"turn_hi{h}") for h in range(2)]
        turn_lo = [sem(f"turn_lo{h}") for h in range(2)]
        w_hi_done = [sem(f"w_hi_done{b}") for b in range(2)]
        w_lo_done = [sem(f"w_lo_done{b}") for b in range(2)]
        g_ready = [sem(f"g_ready{c}") for c in range(2)]
        g_hi_done = [sem(f"g_hi_done{c}") for c in range(2)]
        g_lo_done = [sem(f"g_lo_done{c}") for c in range(2)]
        aw_ready = [sem(f"aw_ready{c}") for c in range(2)]
        router = sem("router")
        e2_ready = sem("e2_ready")
        gates_ready = sem("gates_ready")
        hg_ready = sem("hg_ready")
        hgt_ready = sem("hgt_ready")
        hgt_hi_done = sem("hgt_hi_done")
        hgt_lo_done = sem("hgt_lo_done")
        hgt_stored = sem("hgt_stored")
        logits_ready = sem("logits_ready")
        soft = sem("soft")
        exp_done = sem("exp_done")
        hit_ready = sem("hit_ready")
        count_ready = sem("count_ready")
        csel_ready = sem("csel_ready")
        mask_ready = sem("mask_ready")
        mask_done = sem("mask_done")
        hx_hi_done = sem("hx_hi_done")
        hx_lo_done = sem("hx_lo_done")
        x_kept = [sem(f"x_kept{b}") for b in range(2)]
        main_ready = [sem(f"main_ready{b}") for b in range(2)]
        added = [sem(f"added{b}") for b in range(2)]
        masked = sem("masked")
        result_done = [sem(f"result_done{b}") for b in range(2)]

        ROUTER_STEPS = 13
        SOFT_STEPS = 7

        block = ctx.enter_context(nc.Block())

        @block.sync
        def _(sp):
            def load_w(buf, visit, d):
                if not (isinstance(visit, int) and visit == 0):
                    sp.wait_ge(w_hi_done[buf], visit)
                    sp.wait_ge(w_lo_done[buf], visit)
                if d is None:
                    sp.dma_start(b_view(wraw[buf]), B_t).then_inc(w_landed[buf], 16)
                else:
                    sp.dma_start(wraw[buf][:], W_t[:, :, bass.ts(d, P)]).then_inc(w_landed[buf], 16)

            def load_x(buf, tile):
                sp.dma_start(xraw[buf][:], x_t[bass.ts(tile, P), :]).then_inc(x_landed[buf], 16)

            sp.dma_start(cent_raw[:], cent).then_inc(cent_landed, 16)
            for v in range(V1_TURNS):
                sp.dma_start(vraw[v][0:V1_ROWS, :], V[v * V1_ROWS:(v + 1) * V1_ROWS, :]).then_inc(v_landed[v], 16)
            load_w(0, 0, None)
            load_w(1, 0, 0)

            with sp.Fori(0, V2_TURNS // 2) as i:
                for s in range(2):
                    sp.wait_ge(turned[1], 2 * i + s + 3)
                    sp.dma_start(vraw[s][0:V2_ROWS, :],
                                 V[bass.ds(V2_ROWS * (2 * i + s) + F1, V2_ROWS), :]).then_inc(v_landed[s], 16)
                    load_w(s, i + 1, 2 * i + s + 1)
            sp.dma_start(a_raw[:], A.rearrange("e r d -> (e r) d")).then_inc(small_landed, 16)
            sp.dma_start(wr_raw[:], Wr).then_inc(small_landed, 16)
            sp.dma_start(ids_raw[:], ids.partition_broadcast(P)).then_inc(assign_landed, 16)
            sp.dma_start(as_raw[:], assign.partition_broadcast(C)).then_inc(assign_landed, 16)
            load_w(0, KD // 2, KD - 1)
            load_w(1, KD // 2, None)

            sp.wait_ge(turned[1], TURN_A)
            load_x(0, 0)
            load_x(1, 1)

            def second_sweep(n, buf, visit, tile):
                load_w(buf, visit, n)
                for c in range(2):
                    sp.wait_ge(turned[1], TURN_PAIR + 2 * n + c + 1)
                    load_x(c, tile + c)

            second_sweep(0, 0, 5, 2)
            with sp.Fori(0, NPAIR // 2 - 1) as i:
                second_sweep(2 * i + 1, 1, i + 5, 4 * i + 4)
                second_sweep(2 * i + 2, 0, i + 6, 4 * i + 6)
            second_sweep(NPAIR - 1, 1, 8, 0)

            sp.wait_ge(g_ready[0], G_BASE[0])
            sp.wait_ge(g_ready[1], G_BASE[1])
            sp.dma_start(bias_row[:], bias.partition_broadcast(P)).then_inc(bias_landed, 16)

            def last_stage(i, b, last=False):
                if not last:
                    sp.wait_ge(x_kept[b], i + 1)
                    load_x(b, 2 * i + 2 + b)
                sp.wait_ge(result_done[b], i + 1)
                sp.dma_start(out_t[bass.ts(2 * i + b, P), :], xkeep[b][:]).then_inc(out_stored[b], 16)

            with sp.Fori(0, NPAIR - 1) as i:
                for b in range(2):
                    last_stage(i, b)
            for b in range(2):
                last_stage(NPAIR - 1, b, last=True)
            for b in range(2):
                sp.wait_ge(out_stored[b], 16 * NPAIR)

        @block.gpsimd
        def _(pool):
            nc.gpsimd.memset(ident[:], 0.0).then_inc(const_ready, 1)
            pool.wait_ge(const_ready, 1)
            nc.gpsimd.affine_select(out=ident[:], in_=ident[:], compare_op=ALU.not_equal, fill=1.0, base=0,
                                    pattern=[[-1, P]], channel_multiplier=1).then_inc(const_ready, 1)
            nc.gpsimd.iota(iota8[:], [[1, E]], base=0, channel_multiplier=0,
                           allow_small_or_imprecise_dtypes=True).then_inc(const_ready, 1)
            nc.gpsimd.iota(pidx[:], [[0, 1]], base=0, channel_multiplier=1,
                           allow_small_or_imprecise_dtypes=True).then_inc(const_ready, 1)
            nc.gpsimd.memset(ones_b[:], 1.0).then_inc(const_ready, 1)

        @block.scalar
        def _(act):
            def copy(dst, src):
                return nc.scalar.activation(dst, src, ACT.Copy)

            def turn_to(dst_of_half, number, width=P):
                for h in range(2):
                    act.wait_ge(turned[h], number + 1)
                    copy(dst_of_half(h), ps_turn[:, h, 0:4 * width].rearrange("p (k t) -> p k t", t=width)
                         ).then_inc(turn_hi[h], 1)

            def split_w(buf, visit, is_b=False):
                act.wait_ge(w_landed[buf], 16 * (visit + 1))
                if is_b:
                    copy(b_split_view(w_hi[buf]), b_raw_view(wraw[buf])).then_inc(w_hi_done[buf], 1)
                else:
                    copy(w_hi[buf][:], wraw[buf][:]).then_inc(w_hi_done[buf], 1)

            def xt_half(b):
                return lambda h: xt_hi[b][:, 4 * h:4 * h + 4, :]

            act.wait_ge(small_turned, 1)
            copy(vt1_hi[:, :, F1:HALF], ps_aw[:, 1, :].rearrange("p (k c) -> p k c", c=C)).then_inc(small_hi, 1)
            for v in range(V1_TURNS):
                turn_to(lambda h: vt1_hi[:, 4 * h:4 * h + 4, v * V1_ROWS:(v + 1) * V1_ROWS], v, V1_ROWS)
            split_w(0, 0, is_b=True)

            def g_block(m, bank, visit):
                act.wait_ge(g_ready[bank], visit + 1)
                copy(g_hi[:, bass.ds(m, 1), 0:F1].rearrange("p a f -> p (a f)"), ps_g[bank][:, 0:F1])
                dst = gb_hi[:] if isinstance(m, int) and m == 0 else \
                    aw_hi[:, bass.ds(m - 1, 1), AW:AWG].rearrange("p a c -> p (a c)")
                copy(dst, ps_g[bank][:, F1:HALF]).then_inc(g_hi_done[bank], 1)

            split_w(1, 0)
            g_block(0, 0, 0)
            with act.Fori(0, V2_TURNS // 2) as i:
                for s in range(2):
                    act.wait_ge(g_ready[s], i + 1)
                    split_w(s, i + 1)
                    turn_to(lambda h: vt2_hi[:, 4 * h:4 * h + 4, bass.ts(2 * i + s, V2_ROWS)],
                            TURN_V2 + 2 * i + s, V2_ROWS)
                    g_block(2 * i + s + 1, 1 - s, i + s)
            act.wait_ge(g_ready[0], KD // 2)
            split_w(0, KD // 2)
            turn_to(lambda h: aw_hi[:, 4 * h:4 * h + 4, 0:ER], TURN_A)
            act.wait_ge(small_turned, 2)
            copy(aw_hi[:, :, ER:AW], ps_aw[:, 0, 0:KD * E].rearrange("p (k e) -> p k e", e=E)).then_inc(small_hi, 1)
            g_block(KD - 1, 1, KD // 2 - 1)
            act.wait_ge(g_ready[1], KD // 2)
            split_w(1, KD // 2, is_b=True)
            g_block(KD, 0, KD // 2)

            def g_chunk(c, m):
                act.wait_ge(g_ready[c], G_BASE[c] + m + 1)
                copy(g_hi[:, bass.ds(m, 1), F1 + c * CH:F1 + (c + 1) * CH].rearrange("p a f -> p (a f)"),
                     ps_g[c][:, 0:CH]).then_inc(g_hi_done[c], 1)

            def router_exp(n):
                act.wait_ge(router, ROUTER_STEPS * n + 7)
                nc.scalar.activation(e2[:], diff[:], ACT.Exp).then_inc(e2_ready, 1)

            def split_hgt(n):
                act.wait_ge(hgt_ready, n + 1)
                copy(hgt_hi[:], ps_hgt).then_inc(hgt_hi_done, 1)

            def softmax_exp(n):
                act.wait_ge(soft, SOFT_STEPS * n + 2)
                for c in range(2):
                    nc.scalar.activation(ex[:, c, :], ps_aw[:, c, AW:AWG], ACT.Exp, bias=negb[:, c:c + 1],
                                         scale=1.0 / TEMPERATURE, accum_out=esum[:, c:c + 1]).then_inc(exp_done, 1)

            def second_sweep(n, buf, visit):
                first = isinstance(n, int) and n == 0
                if not first:
                    router_exp(n - 1)
                    act.wait_ge(aw_ready[0], n)
                turn_to(xt_half(0), TURN_PAIR + 2 * n)
                if not first:
                    split_hgt(n - 1)
                    softmax_exp(n - 1)
                    act.wait_ge(aw_ready[1], n)
                turn_to(xt_half(1), TURN_PAIR + 2 * n + 1)
                if first:
                    act.wait_ge(g_ready[0], G_BASE[0])
                else:
                    act.wait_ge(g_ready[1], G_BASE[1] + n)
                split_w(buf, visit)
                for c in range(2):
                    g_chunk(c, n)

            second_sweep(0, 0, 5)
            with act.Fori(0, NPAIR // 2 - 1) as i:
                second_sweep(2 * i + 1, 1, i + 5)
                second_sweep(2 * i + 2, 0, i + 6)
            second_sweep(NPAIR - 1, 1, 8)
            router_exp(NPAIR - 1)
            act.wait_ge(aw_ready[0], NPAIR)
            turn_to(xt_half(0), TURN_MAIN)
            split_hgt(NPAIR - 1)
            softmax_exp(NPAIR - 1)
            for c in range(2):
                g_chunk(c, KD)

            def split_hg(b, tile):
                copy(hx_hi[b][:], hgt_all[:, bass.ts(tile, P)]).then_inc(hx_hi_done, 1)

            def keep(i, b):
                act.wait_ge(x_landed[b], 16 * (NPAIR + 1 + i))
                copy(xkeep[b][:], xraw[b][:]).then_inc(x_kept[b], 1)

            act.wait_ge(hgt_stored, NPAIR)
            split_hg(0, 0)
            keep(0, 0)
            act.wait_ge(mask_ready, 1)
            copy(mask_row[:].rearrange("p (c f) -> p c f", c=2), ps_aw[:]).then_inc(mask_done, 1)

            turn_to(xt_half(1), TURN_MAIN + 1)
            split_hg(1, 1)
            keep(0, 1)
            with act.Fori(1, NPAIR) as i:
                for b in range(2):
                    act.wait_ge(main_ready[b], i)
                    turn_to(xt_half(b), TURN_MAIN + 2 * i + b)
                    split_hg(b, 2 * i + b)
                    act.wait_ge(out_stored[b], 16 * i)
                    keep(i, b)

        @block.vector
        def _(dve):
            def rest(dst, src, hi):
                return nc.vector.tensor_tensor(dst, src, hi.bitcast(F32), ALU.subtract)

            def turn_to(hi_of_half, lo_of_half, number, width=P):
                for h in range(2):
                    dve.wait_ge(turn_hi[h], number + 1)
                    rest(lo_of_half(h), ps_turn[:, h, 0:4 * width].rearrange("p (k t) -> p k t", t=width),
                         hi_of_half(h)).then_inc(turn_lo[h], 1)

            def split_w(buf, visit, is_b=False):
                dve.wait_ge(w_hi_done[buf], visit + 1)
                if is_b:
                    rest(b_split_view(w_lo[buf]), b_raw_view(wraw[buf]),
                         b_split_view(w_hi[buf])).then_inc(w_lo_done[buf], 1)
                else:
                    rest(w_lo[buf][:], wraw[buf][:], w_hi[buf][:]).then_inc(w_lo_done[buf], 1)

            def turn_x(b, number):
                turn_to(lambda h: xt_hi[b][:, 4 * h:4 * h + 4, :], lambda h: xt_lo[b][:, 4 * h:4 * h + 4, :], number)

            dve.wait_ge(small_hi, 1)
            rest(vt1_lo[:, :, F1:HALF], ps_aw[:, 1, :].rearrange("p (k c) -> p k c", c=C),
                 vt1_hi[:, :, F1:HALF]).then_inc(small_lo, 1)
            for v in range(V1_TURNS):
                turn_to(lambda h: vt1_hi[:, 4 * h:4 * h + 4, v * V1_ROWS:(v + 1) * V1_ROWS],
                        lambda h: vt1_lo[:, 4 * h:4 * h + 4, v * V1_ROWS:(v + 1) * V1_ROWS], v, V1_ROWS)
            split_w(0, 0, is_b=True)

            def g_block(m, bank, visit):
                dve.wait_ge(g_hi_done[bank], visit + 1)
                at = (slice(None), bass.ds(m, 1), slice(0, F1))
                rest(g_lo[at].rearrange("p a f -> p (a f)"), ps_g[bank][:, 0:F1],
                     g_hi[at].rearrange("p a f -> p (a f)"))
                if isinstance(m, int) and m == 0:
                    lo, hi = gb_lo[:], gb_hi[:]
                else:
                    at = (slice(None), bass.ds(m - 1, 1), slice(AW, AWG))
                    lo, hi = (t[at].rearrange("p a c -> p (a c)") for t in (aw_lo, aw_hi))
                rest(lo, ps_g[bank][:, F1:HALF], hi).then_inc(g_lo_done[bank], 1)

            split_w(1, 0)
            g_block(0, 0, 0)
            with dve.Fori(0, V2_TURNS // 2) as i:
                for s in range(2):
                    split_w(s, i + 1)
                    turn_to(lambda h: vt2_hi[:, 4 * h:4 * h + 4, bass.ts(2 * i + s, V2_ROWS)],
                            lambda h: vt2_lo[:, 4 * h:4 * h + 4, bass.ts(2 * i + s, V2_ROWS)],
                            TURN_V2 + 2 * i + s, V2_ROWS)
                    g_block(2 * i + s + 1, 1 - s, i + s)
            split_w(0, KD // 2)
            turn_to(lambda h: aw_hi[:, 4 * h:4 * h + 4, 0:ER], lambda h: aw_lo[:, 4 * h:4 * h + 4, 0:ER], TURN_A)
            dve.wait_ge(small_hi, 2)
            rest(aw_lo[:, :, ER:AW], ps_aw[:, 0, 0:KD * E].rearrange("p (k e) -> p k e", e=E),
                 aw_hi[:, :, ER:AW]).then_inc(small_lo, 1)
            g_block(KD - 1, 1, KD // 2 - 1)
            split_w(1, KD // 2, is_b=True)

            dve.wait_ge(const_ready, 5)
            dve.wait_ge(assign_landed, 32)
            nc.vector.memset(hit_sum[:], 0.0).then_inc(setup_step, 1)
            nc.vector.tensor_tensor(lang_bias[:], ids_raw[:].unsqueeze(2).broadcast_to([P, NB, E]),
                                    iota8[:].unsqueeze(1).broadcast_to([P, NB, E]),
                                    ALU.is_equal).then_inc(setup_step, 1)
            nc.vector.tensor_scalar(as_neg[:], as_raw[:], 0.0, float(C), ALU.is_lt, ALU.mult).then_inc(setup_step, 1)
            dve.wait_ge(setup_step, 3)
            nc.vector.tensor_scalar(lang_bias[:], lang_bias[:], LANG_BIAS, None, ALU.mult).then_inc(setup_step, 1)
            nc.vector.tensor_tensor(as_neg[:], as_raw[:], as_neg[:], ALU.add).then_inc(setup_step, 1)
            dve.wait_ge(setup_step, 5)
            nc.vector.tensor_scalar(as_neg[:], as_neg[:], 0.0, float(C - 1), ALU.max, ALU.min).then_inc(setup_step, 1)
            dve.wait_ge(setup_step, 6)
            nc.vector.tensor_scalar(onehot_a[:], as_neg[:], pidx[0:C, :], None, ALU.is_equal).then_inc(setup_step, 1)
            dve.wait_ge(setup_step, 7)
            g_block(KD, 0, KD // 2)

            def g_chunk(c, m):
                dve.wait_ge(g_hi_done[c], G_BASE[c] + m + 1)
                at = (slice(None), bass.ds(m, 1), slice(F1 + c * CH, F1 + (c + 1) * CH))
                rest(g_lo[at].rearrange("p a f -> p (a f)"), ps_g[c][:, 0:CH],
                     g_hi[at].rearrange("p a f -> p (a f)")).then_inc(g_lo_done[c], 1)

            def route(n):
                base = ROUTER_STEPS * n
                dve.wait_ge(aw_ready[1], n + 1)
                def biased(c):
                    nc.vector.tensor_tensor(rl[:, c, :], ps_aw[:, c, ER:AW],
                                            lang_bias[:, bass.ds(n, 1), :].rearrange("p a e -> p (a e)"),
                                            ALU.add).then_inc(router, 1)

                def gap(c):
                    nc.vector.tensor_tensor(diff[:, c:c + 1], m8[:, c, 1:2], m8[:, c, 0:1],
                                            ALU.subtract).then_inc(router, 1)

                biased(0)
                dve.wait_ge(router, base + 1)
                biased(1)
                nc.vector.max(m8[:, 0, :], rl[:, 0, :]).then_inc(router, 1)
                dve.wait_ge(router, base + 3)
                gap(0)
                nc.vector.max(m8[:, 1, :], rl[:, 1, :]).then_inc(router, 1)
                nc.vector.max_index(idx8[:, 0, :], m8[:, 0, :], rl[:, 0, :]).then_inc(router, 1)
                dve.wait_ge(router, base + 5)
                gap(1)
                nc.vector.max_index(idx8[:, 1, :], m8[:, 1, :], rl[:, 1, :]).then_inc(router, 1)
                dve.wait_ge(router, base + 8)
                nc.vector.tensor_tensor(pick[:], iota8[:].unsqueeze(1).unsqueeze(1).broadcast_to([P, 2, 2, E]),
                                        idx8[:, :, 0:2].unsqueeze(3).broadcast_to([P, 2, 2, E]),
                                        ALU.is_equal).then_inc(router, 1)
                dve.wait_ge(e2_ready, n + 1)
                nc.vector.tensor_scalar(den[:], e2[:], 1.0, 1.0 / SCALING, ALU.add, ALU.mult).then_inc(router, 1)
                dve.wait_ge(router, base + 10)
                nc.vector.reciprocal(wts[:, :, 0], den[:]).then_inc(router, 1)
                dve.wait_ge(router, base + 11)
                nc.vector.tensor_tensor(wts[:, :, 1], wts[:, :, 0], e2[:], ALU.mult).then_inc(router, 1)
                dve.wait_ge(router, base + 12)
                nc.vector.tensor_tensor(pick[:], pick[:], wts[:].unsqueeze(3).broadcast_to([P, 2, 2, E]),
                                        ALU.mult).then_inc(router, 1)
                dve.wait_ge(router, base + 13)
                nc.vector.tensor_tensor(gates[:], pick[:, :, 0, :], pick[:, :, 1, :],
                                        ALU.add).then_inc(gates_ready, 1)
                dve.wait_ge(gates_ready, n + 1)
                nc.vector.tensor_tensor(hg[:].rearrange("p c (e r) -> p c e r", r=R),
                                        ps_aw[:, :, 0:ER].rearrange("p c (e r) -> p c e r", r=R),
                                        gates[:].unsqueeze(3).broadcast_to([P, 2, E, R]),
                                        ALU.mult).then_inc(hg_ready, 1)

            def split_hgt(n):
                dve.wait_ge(hgt_hi_done, n + 1)
                rest(hgt_lo[:], ps_hgt, hgt_hi[:]).then_inc(hgt_lo_done, 1)
                nc.vector.tensor_copy(hgt_all[:, bass.ts(n, 2 * P)], ps_hgt).then_inc(hgt_stored, 1)

            def softmax_max(n):
                dve.wait_ge(logits_ready, n + 1)
                nc.vector.tensor_reduce(mx[:], ps_aw[:, :, AW:AWG], AX_X, ALU.max).then_inc(soft, 1)
                dve.wait_ge(soft, SOFT_STEPS * n + 1)
                nc.vector.tensor_scalar(negb[:], mx[:], -1.0 / TEMPERATURE, None, ALU.mult).then_inc(soft, 1)

            def softmax_hits(n):
                dve.wait_ge(exp_done, 2 * n + 2)
                nc.vector.reciprocal(rsum[:], esum[:]).then_inc(soft, 1)
                dve.wait_ge(soft, SOFT_STEPS * n + 3)
                for c in range(2):
                    nc.vector.tensor_scalar(hits[:, c, :], ex[:, c, :], rsum[:, c:c + 1], THRESHOLD,
                                            ALU.mult, ALU.is_gt).then_inc(soft, 1)
                dve.wait_ge(soft, SOFT_STEPS * n + 5)
                nc.vector.tensor_reduce(qsel[:, bass.ts(n, 2)], hits[:], AX_X, ALU.max).then_inc(soft, 1)
                nc.vector.tensor_tensor(hit_sum[:], hit_sum[:], hits[:], ALU.add).then_inc(soft, 1)

            def second_sweep(n, buf, visit):
                first = isinstance(n, int) and n == 0
                if not first:
                    route(n - 1)
                turn_x(0, TURN_PAIR + 2 * n)
                if not first:
                    split_hgt(n - 1)
                    softmax_max(n - 1)
                turn_x(1, TURN_PAIR + 2 * n + 1)
                if not first:
                    softmax_hits(n - 1)
                split_w(buf, visit)
                for c in range(2):
                    g_chunk(c, n)

            second_sweep(0, 0, 5)
            with dve.Fori(0, NPAIR // 2 - 1) as i:
                second_sweep(2 * i + 1, 1, i + 5)
                second_sweep(2 * i + 2, 0, i + 6)
            second_sweep(NPAIR - 1, 1, 8)
            route(NPAIR - 1)
            turn_x(0, TURN_MAIN)
            split_hgt(NPAIR - 1)
            softmax_max(NPAIR - 1)
            softmax_hits(NPAIR - 1)
            dve.wait_ge(soft, SOFT_STEPS * NPAIR)
            nc.vector.tensor_copy(hit_b[:], hit_sum[:]).then_inc(hit_ready, 1)
            for c in range(2):
                g_chunk(c, KD)

            def split_hg(b, tile):
                dve.wait_ge(hx_hi_done, tile + 1)
                rest(hx_lo[b][:], hgt_all[:, bass.ts(tile, P)], hx_hi[b][:]).then_inc(hx_lo_done, 1)

            split_hg(0, 0)
            dve.wait_ge(count_ready, 1)
            nc.vector.tensor_scalar(csel[:], ps_aw[0:C, 0, 0:P], 0.0, None, ALU.is_gt).then_inc(csel_ready, 1)

            def finish(b, i):
                tile = 2 * i + b
                dve.wait_ge(main_ready[b], i + 1)
                nc.vector.tensor_tensor(dense[:], ps_out[:, b, :], bias_row[:], ALU.add).then_inc(added[b], 1)
                dve.wait_ge(added[b], i + 1)
                nc.vector.scalar_tensor_tensor(out=dense[:], in0=dense[:], scalar=qsel[:, bass.ds(tile, 1)],
                                               in1=mask_row[:], op0=ALU.mult, op1=ALU.mult).then_inc(masked, 1)
                dve.wait_ge(masked, tile + 1)
                dve.wait_ge(x_kept[b], i + 1)
                nc.vector.tensor_tensor(xkeep[b][:], dense[:], xkeep[b][:], ALU.add).then_inc(result_done[b], 1)

            turn_x(1, TURN_MAIN + 1)
            split_hg(1, 1)
            dve.wait_ge(mask_done, 1)
            dve.wait_ge(bias_landed, 16)
            finish(0, 0)
            with dve.Fori(1, NPAIR) as i:
                turn_x(0, TURN_MAIN + 2 * i)
                split_hg(0, 2 * i)
                dve.wait_ge(result_done[0], i)
                finish(1, i - 1)
                turn_x(1, TURN_MAIN + 2 * i + 1)
                split_hg(1, 2 * i + 1)
                dve.wait_ge(result_done[1], i)
                finish(0, i)
            dve.wait_ge(result_done[0], NPAIR)
            finish(1, NPAIR - 1)

        @block.tensor
        def _(pe):
            def turn(src_of_k, number, rows=P):
                for h in range(2):
                    if not (isinstance(number, int) and number == 0):
                        pe.wait_ge(turn_lo[h], number)
                    for k in range(4):
                        last = nc.tensor.transpose(ps_turn[:, h, k * rows:(k + 1) * rows], src_of_k(4 * h + k),
                                                   ident[0:rows, 0:rows])
                    last.then_inc(turned[h], 1)

            def turn_v(buf, rows, number):
                turn(lambda j: vraw[buf][0:rows, j::KO], number, rows)

            def turn_tile(b, visit, number):
                pe.wait_ge(x_landed[b], 16 * (visit + 1))
                turn(lambda k: xraw[b][:, k * P:(k + 1) * P], number)

            def product(dst, left, right, j0=0, j1=KO):
                for j in range(j0, j1):
                    l_hi, l_lo = left(j)
                    r_hi, r_lo = right(j)
                    nc.tensor.matmul(dst, l_hi, r_hi, start=(j == 0), stop=False)
                    nc.tensor.matmul(dst, l_hi, r_lo, start=False, stop=False)
                    last = nc.tensor.matmul(dst, l_lo, r_hi, start=False, stop=(j == KO - 1))
                return last

            pe.wait_ge(const_ready, 2)
            pe.wait_ge(cent_landed, 16)
            for j in range(KO):
                last = nc.tensor.transpose(ps_aw[:, 1, j * C:(j + 1) * C], cent_raw[:, j::KO], ident[0:C, 0:C])
            last.then_inc(small_turned, 1)
            for v in range(V1_TURNS):
                pe.wait_ge(v_landed[v], 16)
                turn_v(v, V1_ROWS, v)

            def g_part(buf, bank, j0, j1):
                return product(ps_g[bank], lambda j: (w_hi[buf][:, j, :], w_lo[buf][:, j, :]),
                               lambda j: (vt1_hi[:, j, :], vt1_lo[:, j, :]), j0, j1)

            def first_sweep_step(buf, visit, turn_between=None):
                pe.wait_ge(w_lo_done[buf], visit + 1)
                if not (isinstance(visit, int) and visit == 0):
                    pe.wait_ge(g_lo_done[buf], visit)
                g_part(buf, buf, 0, 4)
                if turn_between is not None:
                    turn_between()
                g_part(buf, buf, 4, KO).then_inc(g_ready[buf], 1)

            def turn_a():
                pe.wait_ge(small_landed, 32)
                turn(lambda k: a_raw[:, k * P:(k + 1) * P], TURN_A)
                for k in range(KD):
                    last = nc.tensor.transpose(ps_aw[:, 0, k * E:(k + 1) * E], wr_raw[:, k * P:(k + 1) * P],
                                               ident[0:E, 0:E])
                last.then_inc(small_turned, 1)

            pe.wait_ge(small_lo, 1)
            for h in range(2):
                pe.wait_ge(turn_lo[h], TURN_V2)
            first_sweep_step(0, 0)

            def v2_turn(i, s):
                pe.wait_ge(v_landed[s], 16 * (i + 2))
                turn_v(s, V2_ROWS, TURN_V2 + 2 * i + s)

            pe.wait_ge(w_lo_done[1], 1)
            g_part(1, 1, 0, 4)
            v2_turn(0, 0)
            g_part(1, 1, 4, KO).then_inc(g_ready[1], 1)
            first_sweep_step(0, 1, lambda: v2_turn(0, 1))
            with pe.Fori(1, V2_TURNS // 2) as i:
                first_sweep_step(1, i, lambda: v2_turn(i, 0))
                first_sweep_step(0, i + 1, lambda: v2_turn(i, 1))
            first_sweep_step(1, KD // 2 - 1, turn_a)
            first_sweep_step(0, KD // 2)

            def g_chunk(buf, c, j0, j1):
                return product(ps_g[c][:, 0:CH], lambda j: (w_hi[buf][:, j, :], w_lo[buf][:, j, :]),
                               lambda j: (vt2_hi[:, j, c * CH:(c + 1) * CH], vt2_lo[:, j, c * CH:(c + 1) * CH]),
                               j0, j1)

            def token_product(c, number):
                for h in range(2):
                    pe.wait_ge(turn_lo[h], number + 1)
                last = product(ps_aw[:, c, 0:AWG], lambda k: (xt_hi[c][:, k, :], xt_lo[c][:, k, :]),
                               lambda k: (aw_hi[:, k, :], aw_lo[:, k, :]))
                last.then_inc(aw_ready[c], 1)

            def turn_hg(n):
                pe.wait_ge(hg_ready, n + 1)
                if not (isinstance(n, int) and n == 0):
                    pe.wait_ge(hgt_stored, n)
                for c in range(2):
                    last = nc.tensor.transpose(ps_hgt[:, c * P:(c + 1) * P], hg[:, c, :], ident[:])
                last.then_inc(hgt_ready, 1)

            def lora_logits(n):
                pe.wait_ge(hgt_lo_done, n + 1)
                for c in range(2):
                    for hl, gb in ((hgt_hi, gb_hi), (hgt_hi, gb_lo), (hgt_lo, gb_hi)):
                        last = nc.tensor.matmul(ps_aw[:, c, AW:AWG], hl[:, c * P:(c + 1) * P], gb[:],
                                                start=False, stop=True, skip_group_check=True)
                last.then_inc(logits_ready, 1)

            def second_sweep(n, buf, visit, prev=None, tokens=True):
                if tokens:
                    turn_tile(0, n, TURN_PAIR + 2 * n)
                else:
                    turn_tile(0, NPAIR, TURN_MAIN)
                pe.wait_ge(w_lo_done[buf], visit + 1)
                pe.wait_ge(g_lo_done[0], G_BASE[0] + n)
                g_chunk(buf, 0, 0, 6)
                if prev is not None:
                    turn_hg(prev)
                last = g_chunk(buf, 0, 6, KO)
                last.then_inc(g_ready[0], 1)
                pe.wait_ge(g_lo_done[1], G_BASE[1] + n)
                g_chunk(buf, 1, 0, 1)
                if prev is not None:
                    lora_logits(prev)
                if tokens:
                    turn_tile(1, n, TURN_PAIR + 2 * n + 1)
                g_chunk(buf, 1, 1, 4)
                if tokens:
                    if prev is not None:
                        pe.wait_ge(exp_done, 2 * n)
                    token_product(0, TURN_PAIR + 2 * n)
                g_chunk(buf, 1, 4, KO).then_inc(g_ready[1], 1)
                if tokens:
                    token_product(1, TURN_PAIR + 2 * n + 1)

            pe.wait_ge(small_lo, 2)
            for h in range(2):
                pe.wait_ge(turn_lo[h], TURN_PAIR)
                pe.wait_ge(g_lo_done[h], G_BASE[h])
            second_sweep(0, 1, 4)
            second_sweep(1, 0, 5, 0)
            second_sweep(2, 1, 5, 1)
            with pe.Fori(1, NPAIR // 2 - 1) as i:
                second_sweep(2 * i + 1, 0, i + 5, 2 * i)
                second_sweep(2 * i + 2, 1, i + 5, 2 * i + 1)
            second_sweep(NPAIR - 1, 0, 8, NPAIR - 2)
            second_sweep(KD, 1, 8, NPAIR - 1, tokens=False)

            pe.wait_ge(hit_ready, 1)
            for c in range(2):
                last = nc.tensor.matmul(ps_aw[0:C, 0, 0:P], hit_b[:, c, :], ones_b[:], start=(c == 0), stop=(c == 1))
            last.then_inc(count_ready, 1)

            def column_mask():
                pe.wait_ge(csel_ready, 1)
                for c in range(2):
                    last = nc.tensor.matmul(ps_aw[:, c, :], csel[:], onehot_a[:, c * HALF:(c + 1) * HALF],
                                            start=True, stop=True)
                last.then_inc(mask_ready, 1)

            def main_tile(b, i, first=False, last_tile=False):
                tile = 2 * i + b
                for h in range(2):
                    pe.wait_ge(turn_lo[h], TURN_MAIN + tile + 1)
                if not first:
                    pe.wait_ge(added[b], i)
                for k in range(KG):
                    l_hi = xt_hi[b][:, k, :] if k < KD else hx_hi[b][:]
                    l_lo = xt_lo[b][:, k, :] if k < KD else hx_lo[b][:]
                    r = k + 1 if k < KD else 0
                    if k == KD:
                        pe.wait_ge(hx_lo_done, tile + 1)
                    for g in (g_hi, g_lo):
                        for c in range(2):
                            nc.tensor.matmul(ps_out[:, b, c * HALF:(c + 1) * HALF], l_hi,
                                             g[:, r, c * HALF:(c + 1) * HALF], start=k == 0 and g is g_hi, stop=False)
                    for c in range(2):
                        last = nc.tensor.matmul(ps_out[:, b, c * HALF:(c + 1) * HALF], l_lo,
                                                g_hi[:, r, c * HALF:(c + 1) * HALF], start=False, stop=k == KD)
                    if k == 1 and first and b == 0:
                        column_mask()
                    if k == 3 and not last_tile:
                        turn_tile(1 - b, NPAIR + i + b, TURN_MAIN + tile + 1)
                last.then_inc(main_ready[b], 1)

            for c in range(2):
                pe.wait_ge(g_lo_done[c], G_BASE[c] + KG)
            pe.wait_ge(hgt_stored, NPAIR)
            main_tile(0, 0, first=True)
            main_tile(1, 0, first=True)
            with pe.Fori(1, NPAIR - 1) as i:
                for b in range(2):
                    main_tile(b, i)
            main_tile(0, NPAIR - 1)
            main_tile(1, NPAIR - 1, last_tile=True)


_INS = ["x", "itok_B_0_7", "L0_cond_W", "L0_cond_Wr", "L0_cond_A", "L0_cond_B",
        "L0_ffn_weight", "L0_ffn_bias", "L0_ffn_centroids", "L0_ffn_assignments"]


def kernel(**inputs):
    import numpy as np
    import concourse.bacc as bacc
    from concourse.bass_utils import run_bass_kernel_spmd

    nc = bacc.Bacc("TRN2", target_bir_lowering=False, num_devices=1)
    arrays, args = {}, []
    for name in _INS:
        a = np.ascontiguousarray(inputs[name])
        arrays[f"in_{name}"] = a
        args.append(nc.dram_tensor(f"in_{name}", a.shape, mybir.dt.from_np(a.dtype), kind="ExternalInput").ap())
    shape = inputs["x"].shape
    out = nc.dram_tensor("out_0", shape, F32, kind="ExternalOutput").ap()
    adaln_ffn_kernel(nc, *args, out)
    r = run_bass_kernel_spmd(nc, [arrays], core_ids=[0])
    return r.results[0]["out_0"]
```

```python
from contextlib import ExitStack

import concourse.bass as bass
from concourse import mybir

ALU = mybir.AluOpType
ACT = mybir.ActivationFunctionType
AX_X = mybir.AxisListType.X
F32 = mybir.dt.float32
F32R = mybir.dt.float32r
BF16 = mybir.dt.bfloat16
I32 = mybir.dt.int32
U32 = mybir.dt.uint32

P = 128
HALF = 512
LANG_BIAS = 5.0
SCALING = 2.0
THRESHOLD = 0.01
TEMPERATURE = 0.1



def adaln_ffn_kernel(nc, x, ids, W, Wr, A, B, V, bias, cent, assign, out):
    NB, S, D = x.shape
    O = W.shape[0]
    E, R, _ = A.shape
    C = cent.shape[0]
    FO = V.shape[0]
    ER = E * R
    T = NB * S
    NT = T // P
    NPAIR = NT // 2
    KD = D // P
    KO = O // P
    KG = KD + 1
    AW = ER + E
    AWG = AW + C
    LO_A, LO_WR = AWG + C, AWG + C + ER
    F1 = HALF - C
    F2 = FO - F1
    CH = F2 // 2
    V1_TURNS, V2_TURNS = 4, KD - 2
    V1_ROWS, V2_ROWS = F1 // V1_TURNS, F2 // V2_TURNS
    TURN_V2 = V1_TURNS
    TURN_A = TURN_V2 + V2_TURNS
    TURN_PAIR = TURN_A + 1
    G_BASE = [(KG + 1) // 2, KG // 2]
    BANK = [1, 0]
    assert S == 2 * P and ER == P and KD == KO == NPAIR == 8 and FO == 2 * HALF and C < P and E <= 8

    x_t = x.rearrange("b s d -> (b s) d")
    out_t = out.rearrange("b s d -> (b s) d")
    W_t = W.rearrange("(p j) d -> p j d", j=KO)
    B_t = B.rearrange("e (p j) r -> p e (j r)", j=KO)
    xt_dram = nc.dram_tensor("xt_scratch", [NT * P, D], F32, kind="Internal").ap()

    def b_view(raw):
        return raw[:].rearrange("p (e a) b -> p e (a b)", e=E)

    def b_raw_view(raw):
        return raw[:].rearrange("p e (j r) -> p j e r", r=R)

    def b_split_view(split):
        return split[:].rearrange("p j (e r) -> p j e r", r=R)

    with ExitStack() as ctx:
        def sb(name, shape, dt, stack=ctx):
            return stack.enter_context(nc.sbuf_tensor(name, shape, dt))

        def sem(name):
            return ctx.enter_context(nc.semaphore(name))

        ident = sb("ident", [P, P], F32)
        aw = sb("aw", [P, KD, 2 * AWG], F32R)
        gb = sb("gb", [P, 2 * C], F32R)
        onehot_a = sb("onehot_a", [C, FO], BF16)
        iota8 = sb("iota8", [P, E], F32)
        pidx = sb("pidx", [P, 1], F32)
        lang_bias = sb("lang_bias", [P, NB, E], F32)
        ones_b = sb("ones_b", [P, P], BF16)
        hit_sum = sb("hit_sum", [P, 2, C], F32)
        hit_b = sb("hit_b", [P, 2, C], BF16)
        csel = sb("csel", [C, P], BF16)
        qsel = sb("qsel", [P, NT], F32)
        rl = sb("rl", [P, 2, E], F32)
        m8 = sb("m8", [P, 2, 8], F32)
        idx8 = sb("idx8", [P, 2, 8], U32)
        diff = sb("diff", [P, 2], F32)
        e2 = sb("e2", [P, 2], F32)
        den = sb("den", [P, 2], F32)
        wts = sb("wts", [P, 2, 2], F32)
        pick = sb("pick", [P, 2, 2, E], F32)
        gates = sb("gates", [P, 2, E], F32)
        hg = sb("hg", [P, 2, ER], F32)
        mx = sb("mx", [P, 2], F32)
        negb = sb("negb", [P, 2], F32)
        ex = sb("ex", [P, 2, C], F32)
        esum = sb("esum", [P, 2], F32)
        rsum = sb("rsum", [P, 2], F32)
        hits = sb("hits", [P, 2, C], F32)

        with ExitStack() as early:
            vraw = [sb(f"vraw{b}", [P, O], F32, early) for b in range(2)]
            as_raw = sb("as_raw", [C, FO], I32, early)
            with ExitStack() as earliest:
                cent_raw = sb("cent_raw", [C, O], F32, earliest)
                vraw += [sb(f"vraw{b}", [P, O], F32, earliest) for b in (2, 3)]
            as_neg = sb("as_neg", [C, FO], F32, early)
            a_raw = sb("a_raw", [ER, D], F32, early)
            wr_raw = sb("wr_raw", [E, D], F32, early)
        xraw = [sb(f"xraw{b}", [P, D], F32) for b in range(2)]
        xt_hi = [sb("xt0_hi", [P, KD, P], F32R), None]
        xt_lo = [sb("xt0_lo", [P, KD, P], F32R), None]
        hgt_all = sb("hgt_all", [P, T], F32)
        ids_raw = sb("ids_raw", [P, NB], I32)

        g_hi = sb("g_hi", [P, KG, FO], F32R)
        g_lo = sb("g_lo", [P, KG, FO], F32R)

        vt2_hi = sb("vt2_hi", [P, KO, F2], F32R)
        vt2_lo = sb("vt2_lo", [P, KO, F2], F32R)
        wraw = [sb(f"wraw{b}", [P, KO, P], F32) for b in range(2)]
        w_hi = [sb(f"w{b}_hi", [P, KO, P], F32R) for b in range(2)]
        w_lo = [sb(f"w{b}_lo", [P, KO, P], F32R) for b in range(2)]
        with ExitStack() as first_sweep:
            vt1_hi = sb("vt1_hi", [P, KO, HALF], F32R, first_sweep)
            vt1_lo = sb("vt1_lo", [P, KO, HALF], F32R, first_sweep)
        xt_hi[1] = sb("xt1_hi", [P, KD, P], F32R)
        xt_lo[1] = sb("xt1_lo", [P, KD, P], F32R)
        hgt_hi = sb("hgt_hi", [P, 2 * P], F32R)
        hgt_lo = sb("hgt_lo", [P, 2 * P], F32R)
        xt_raw = [sb(f"xt_raw{b}", [P, KD, P], F32) for b in range(2)]
        hx_hi = [sb(f"hx{b}_hi", [P, P], F32R) for b in range(2)]
        hx_lo = [sb(f"hx{b}_lo", [P, P], F32R) for b in range(2)]
        bias_row = sb("bias_row", [P, FO], F32)
        mask_row = sb("mask_row", [P, FO], BF16)
        aw_rest = sb("aw_rest", [P, 2, AW], F32)
        logits = sb("logits", [P, 2, C], F32)
        dense = sb("dense", [P, FO], F32)

        ps_turn = ctx.enter_context(nc.psum_tensor("ps_turn", [P, 2, HALF], F32))
        ps_aw = ctx.enter_context(nc.psum_tensor("ps_aw", [P, 2, HALF], F32))
        ps_out = ctx.enter_context(nc.psum_tensor("ps_out", [P, 2, FO], F32))
        ps_g = [ps_out[:, 0, c * HALF:(c + 1) * HALF] for c in range(2)]
        ps_hgt = ps_out[:, 1, 0:2 * P]
        ps_turn_v = [ps_turn, ps_out[:, 1, :].rearrange("p (h f) -> p h f", h=2)]

        LAST_PARTS = [slice(0, HALF), slice(HALF, HALF + HALF // 2), slice(HALF + HALF // 2, FO)]
        ps_last = [ps_out[:, 0, LAST_PARTS[0]], ps_out[:, 0, LAST_PARTS[1]], ps_turn[:, 0, 0:HALF // 2]]

        cent_landed = sem("cent_landed")
        small_landed = sem("small_landed")
        assign_landed = sem("assign_landed")
        bias_landed = sem("bias_landed")
        w_landed = [sem(f"w_landed{b}") for b in range(2)]
        v_landed = [sem(f"v_landed{b}") for b in range(4)]
        x_landed = [sem(f"x_landed{b}") for b in range(2)]
        out_stored = [sem(f"out_stored{b}") for b in range(2)]
        const_ready = sem("const_ready")
        setup_step = sem("setup_step")
        small_turned = sem("small_turned")
        small_hi = sem("small_hi")
        small_lo = sem("small_lo")
        turned = [sem(f"turned{h}") for h in range(2)]
        turn_hi = [sem(f"turn_hi{h}") for h in range(2)]
        turn_lo = [sem(f"turn_lo{h}") for h in range(2)]
        w_hi_done = [sem(f"w_hi_done{b}") for b in range(2)]
        w_lo_done = [sem(f"w_lo_done{b}") for b in range(2)]
        g_ready = [sem(f"g_ready{c}") for c in range(2)]
        g_hi_done = [sem(f"g_hi_done{c}") for c in range(2)]
        g_lo_done = [sem(f"g_lo_done{c}") for c in range(2)]
        aw_ready = [sem(f"aw_ready{c}") for c in range(2)]
        router = sem("router")
        rest_taken = sem("rest_taken")
        logits_rest = sem("logits_rest")
        e2_ready = sem("e2_ready")
        gates_ready = sem("gates_ready")
        hg_ready = sem("hg_ready")
        hgt_ready = sem("hgt_ready")
        hgt_hi_done = sem("hgt_hi_done")
        hgt_lo_done = sem("hgt_lo_done")
        hgt_stored = sem("hgt_stored")
        logits_ready = sem("logits_ready")
        soft = sem("soft")
        exp_done = sem("exp_done")
        hit_ready = sem("hit_ready")
        count_ready = sem("count_ready")
        csel_ready = sem("csel_ready")
        mask_ready = sem("mask_ready")
        mask_done = sem("mask_done")
        xt_kept = [sem(f"xt_kept{b}") for b in range(2)]
        xt_split = [sem(f"xt_split{b}") for b in range(2)]
        xt_hi_done = [sem(f"xt_hi_done{b}") for b in range(2)]
        xt_stored = [sem(f"xt_stored{b}") for b in range(2)]
        xt_landed = [sem(f"xt_landed{b}") for b in range(2)]
        hx_hi_done = sem("hx_hi_done")
        hx_lo_done = sem("hx_lo_done")
        main_ready = [sem(f"main_ready{b}") for b in range(2)]
        added = [sem(f"added{b}") for b in range(2)]
        masked = sem("masked")
        result_done = [sem(f"result_done{b}") for b in range(2)]

        ROUTER_STEPS = 14
        WARM_UP = 17
        SOFT_STEPS = 8

        block = ctx.enter_context(nc.Block())

        @block.sync
        def _(sp):
            def load_w(buf, visit, d):
                if not (isinstance(visit, int) and visit == 0):
                    sp.wait_ge(w_hi_done[buf], visit)
                    sp.wait_ge(w_lo_done[buf], visit)
                if d is None:
                    sp.dma_start(b_view(wraw[buf]), B_t).then_inc(w_landed[buf], 16)
                else:
                    sp.dma_start(wraw[buf][:], W_t[:, :, bass.ts(d, P)]).then_inc(w_landed[buf], 16)

            def load_x(buf, tile):
                sp.dma_start(xraw[buf][:], x_t[bass.ts(tile, P), :]).then_inc(x_landed[buf], 16)

            load_w(0, 0, None)
            for v in range(V1_TURNS):
                sp.dma_start(vraw[v][0:V1_ROWS, :], V[v * V1_ROWS:(v + 1) * V1_ROWS, :]).then_inc(v_landed[v], 16)
                if v == 1:
                    sp.dma_start(cent_raw[:], cent).then_inc(cent_landed, 16)
            load_w(1, 0, 0)

            with sp.Fori(0, V2_TURNS // 2) as i:
                for s in range(2):
                    sp.wait_ge(turned[1], 2 * i + s + 3)
                    sp.dma_start(vraw[s][0:V2_ROWS, :],
                                 V[bass.ds(V2_ROWS * (2 * i + s) + F1, V2_ROWS), :]).then_inc(v_landed[s], 16)
                    load_w(s, i + 1, 2 * i + s + 1)
            sp.dma_start(a_raw[:], A.rearrange("e r d -> (e r) d")).then_inc(small_landed, 16)
            sp.dma_start(wr_raw[:], Wr).then_inc(small_landed, 16)
            sp.dma_start(ids_raw[:], ids.partition_broadcast(P)).then_inc(assign_landed, 16)
            sp.dma_start(as_raw[:], assign.partition_broadcast(C)).then_inc(assign_landed, 16)
            load_w(0, KD // 2, KD - 1)
            load_w(1, KD // 2, None)

            sp.wait_ge(turned[1], TURN_A)
            load_x(0, 0)
            load_x(1, 1)

            def second_sweep(n, buf, visit, last=False):
                load_w(buf, visit, n)
                for c in range(2):
                    sp.wait_ge(turned[1], TURN_PAIR + 2 * n + c + 1)
                    load_x(c, c if last else 2 * n + 2 + c)
                    sp.wait_ge(xt_kept[c], 2 * n + 2)
                    sp.dma_start(xt_dram[bass.ts(2 * n + c, P), :],
                                 xt_raw[c][:].rearrange("p k t -> p (k t)")).then_inc(xt_stored[c], 16)

            second_sweep(0, 0, 5)
            with sp.Fori(0, NPAIR // 2 - 1) as i:
                second_sweep(2 * i + 1, 1, i + 5)
                second_sweep(2 * i + 2, 0, i + 6)
            second_sweep(NPAIR - 1, 1, 8, last=True)

            sp.wait_ge(g_ready[0], G_BASE[0])
            sp.wait_ge(g_ready[1], G_BASE[1])
            sp.dma_start(bias_row[:], bias.partition_broadcast(P)).then_inc(bias_landed, 16)

            def load_xt(b, tile):
                sp.dma_start(xt_raw[b][:].rearrange("p k t -> p (k t)"),
                             xt_dram[bass.ts(tile, P), :]).then_inc(xt_landed[b], 16)

            for b in range(2):
                sp.wait_ge(xt_stored[b], 16 * NPAIR)
                sp.wait_ge(xt_split[b], NPAIR)
                load_xt(b, b)

            def last_stage(i, b):
                sp.wait_ge(xt_split[b], NPAIR + 1 + i)
                load_xt(b, 2 * i + 2 + b)
                sp.wait_ge(result_done[b], i + 1)
                sp.dma_start(out_t[bass.ts(2 * i + b, P), :], xraw[b][:]).then_inc(out_stored[b], 16)

            last_stage(0, 0)
            with sp.Fori(0, NPAIR - 2) as i:
                last_stage(i, 1)
                sp.wait_ge(out_stored[0], 16 * i + 16)
                load_x(0, 2 * i + 2)
                last_stage(i + 1, 0)
                sp.wait_ge(out_stored[1], 16 * i + 16)
                load_x(1, 2 * i + 3)
            last_stage(NPAIR - 2, 1)
            sp.wait_ge(out_stored[0], 16 * (NPAIR - 1))
            load_x(0, NT - 2)
            sp.wait_ge(result_done[0], NPAIR)
            sp.dma_start(out_t[(NT - 2) * P:(NT - 1) * P, :], xraw[0][:]).then_inc(out_stored[0], 16)
            sp.wait_ge(out_stored[1], 16 * (NPAIR - 1))
            load_x(1, NT - 1)
            for c, cols in enumerate(LAST_PARTS):
                sp.wait_ge(result_done[1], NPAIR + c)
                sp.dma_start(out_t[(NT - 1) * P:NT * P, cols], xraw[1][:, cols]).then_inc(out_stored[1], 16)
            sp.wait_ge(out_stored[0], 16 * NPAIR)
            sp.wait_ge(out_stored[1], 16 * (NPAIR - 1 + len(LAST_PARTS)))

        @block.gpsimd
        def _(pool):
            nc.gpsimd.memset(ident[:], 0.0).then_inc(const_ready, 1)
            pool.wait_ge(const_ready, 1)
            nc.gpsimd.affine_select(out=ident[:], in_=ident[:], compare_op=ALU.not_equal, fill=1.0, base=0,
                                    pattern=[[-1, P]], channel_multiplier=1).then_inc(const_ready, 1)
            nc.gpsimd.iota(iota8[:], [[1, E]], base=0, channel_multiplier=0,
                           allow_small_or_imprecise_dtypes=True).then_inc(const_ready, 1)
            nc.gpsimd.iota(pidx[:], [[0, 1]], base=0, channel_multiplier=1,
                           allow_small_or_imprecise_dtypes=True).then_inc(const_ready, 1)
            nc.gpsimd.memset(ones_b[:], 1.0).then_inc(const_ready, 1)

        @block.scalar
        def _(act):
            def copy(dst, src):
                return nc.scalar.activation(dst, src, ACT.Copy)

            def turn_to(dst_of_half, number, width=P, ps=ps_turn):
                for h in range(2):
                    act.wait_ge(turned[h], number + 1)
                    copy(dst_of_half(h), ps[:, h, 0:4 * width].rearrange("p (k t) -> p k t", t=width)
                         ).then_inc(turn_hi[h], 1)

            def turn_tile(b, number):
                for h in range(2):
                    act.wait_ge(turned[h], number + 1)
                    ps = ps_turn[:, h, :].rearrange("p (k t) -> p k t", t=P)
                    copy(xt_raw[b][:, 4 * h:4 * h + 4, :], ps).then_inc(xt_kept[b], 1)
                    copy(xt_hi[b][:, 4 * h:4 * h + 4, :], ps).then_inc(turn_hi[h], 1)

            def split_w(buf, visit, is_b=False):
                act.wait_ge(w_landed[buf], 16 * (visit + 1))
                if is_b:
                    copy(b_split_view(w_hi[buf]), b_raw_view(wraw[buf])).then_inc(w_hi_done[buf], 1)
                else:
                    copy(w_hi[buf][:], wraw[buf][:]).then_inc(w_hi_done[buf], 1)

            split_w(0, 0, is_b=True)
            for v in range(V1_TURNS):
                turn_to(lambda h: vt1_hi[:, 4 * h:4 * h + 4, v * V1_ROWS:(v + 1) * V1_ROWS], v, V1_ROWS,
                        ps_turn_v[v % 2])
                if v == 1:
                    act.wait_ge(small_turned, 1)
                    copy(vt1_hi[:, :, F1:HALF],
                         ps_aw[:, 1, :].rearrange("p (k c) -> p k c", c=C)).then_inc(small_hi, 1)

            def g_block(m, bank, visit):
                act.wait_ge(g_ready[bank], visit + 1)
                copy(g_hi[:, bass.ds(m, 1), 0:F1].rearrange("p a f -> p (a f)"), ps_g[bank][:, 0:F1])
                dst = gb[:, 0:C] if isinstance(m, int) and m == 0 else \
                    aw[:, bass.ds(m - 1, 1), AW:AWG].rearrange("p a c -> p (a c)")
                copy(dst, ps_g[bank][:, F1:HALF]).then_inc(g_hi_done[bank], 1)

            split_w(1, 0)
            g_block(0, 0, 0)
            with act.Fori(0, V2_TURNS // 2) as i:
                for s in range(2):
                    act.wait_ge(g_ready[s], i + 1)
                    split_w(s, i + 1)
                    turn_to(lambda h: vt2_hi[:, 4 * h:4 * h + 4, bass.ts(2 * i + s, V2_ROWS)],
                            TURN_V2 + 2 * i + s, V2_ROWS)
                    g_block(2 * i + s + 1, 1 - s, i + s)
            act.wait_ge(g_ready[0], KD // 2)
            split_w(0, KD // 2)
            turn_to(lambda h: aw[:, 4 * h:4 * h + 4, 0:ER], TURN_A)
            act.wait_ge(small_turned, 2)
            copy(aw[:, :, ER:AW], ps_aw[:, 0, 0:KD * E].rearrange("p (k e) -> p k e", e=E)).then_inc(small_hi, 1)
            g_block(KD - 1, 1, KD // 2 - 1)
            act.wait_ge(g_ready[1], KD // 2)
            split_w(1, KD // 2, is_b=True)
            g_block(KD, 0, KD // 2)

            def g_chunk(c, m):
                bank = BANK[c]
                act.wait_ge(g_ready[bank], G_BASE[bank] + m + 1)
                copy(g_hi[:, bass.ds(m, 1), F1 + c * CH:F1 + (c + 1) * CH].rearrange("p a f -> p (a f)"),
                     ps_g[bank][:, 0:CH]).then_inc(g_hi_done[bank], 1)

            def router_exp(n):
                act.wait_ge(router, ROUTER_STEPS * n + 6)
                nc.scalar.activation(e2[:], diff[:], ACT.Exp).then_inc(e2_ready, 1)

            def take_rest(c, n):
                act.wait_ge(aw_ready[c], n + 1)
                copy(aw_rest[:, c, :], ps_aw[:, c, LO_A:2 * AWG]).then_inc(rest_taken, 1)

            def split_hgt(n):
                act.wait_ge(hgt_ready, n + 1)
                copy(hgt_hi[:], ps_hgt).then_inc(hgt_hi_done, 1)

            def take_logits_rest(n):
                act.wait_ge(logits_ready, n + 1)
                copy(aw_rest[:, :, 0:C], ps_aw[:, :, AWG:AWG + C]).then_inc(logits_rest, 1)

            def softmax_exp(n):
                act.wait_ge(soft, SOFT_STEPS * n + 3)
                for c in range(2):
                    nc.scalar.activation(ex[:, c, :], logits[:, c, :], ACT.Exp, bias=negb[:, c:c + 1],
                                         scale=1.0 / TEMPERATURE, accum_out=esum[:, c:c + 1]).then_inc(exp_done, 1)

            def second_sweep(n, buf, visit):
                first = isinstance(n, int) and n == 0
                if not first:
                    router_exp(n - 1)
                    act.wait_ge(aw_ready[0], n)
                    act.wait_ge(xt_stored[0], 16 * n)
                else:
                    act.wait_ge(setup_step, 7)
                turn_tile(0, TURN_PAIR + 2 * n)
                if not first:
                    split_hgt(n - 1)
                    take_logits_rest(n - 1)
                    act.wait_ge(aw_ready[1], n)
                    act.wait_ge(xt_stored[1], 16 * n)
                turn_tile(1, TURN_PAIR + 2 * n + 1)
                if not first:
                    softmax_exp(n - 1)
                if first:
                    act.wait_ge(g_ready[0], G_BASE[0])
                else:
                    act.wait_ge(g_ready[BANK[1]], G_BASE[BANK[1]] + n)
                split_w(buf, visit)
                for c in range(2):
                    g_chunk(c, n)
                    take_rest(c, n)

            second_sweep(0, 0, 5)
            with act.Fori(0, NPAIR // 2 - 1) as i:
                second_sweep(2 * i + 1, 1, i + 5)
                second_sweep(2 * i + 2, 0, i + 6)
            second_sweep(NPAIR - 1, 1, 8)
            router_exp(NPAIR - 1)

            def split_tile(b, visit, tile):
                act.wait_ge(xt_landed[b], 16 * visit + 16)
                copy(xt_hi[b][:], xt_raw[b][:]).then_inc(xt_hi_done[b], 1)
                copy(hx_hi[b][:], hgt_all[:, bass.ts(tile, P)]).then_inc(hx_hi_done, 1)

            act.wait_ge(aw_ready[0], NPAIR)
            act.wait_ge(hgt_stored, NPAIR - 1)
            split_tile(0, 0, 0)
            split_hgt(NPAIR - 1)
            take_logits_rest(NPAIR - 1)
            softmax_exp(NPAIR - 1)
            g_chunk(0, KD)
            act.wait_ge(aw_ready[1], NPAIR)
            g_chunk(1, KD)
            split_tile(1, 0, 1)
            act.wait_ge(hgt_stored, NPAIR)
            act.wait_ge(mask_ready, 1)
            copy(mask_row[:].rearrange("p (c f) -> p c f", c=2), ps_aw[:]).then_inc(mask_done, 1)
            with act.Fori(1, NPAIR) as i:
                for b in range(2):
                    act.wait_ge(main_ready[b], i)
                    split_tile(b, i, 2 * i + b)

        @block.vector
        def _(dve):
            def rest(dst, src, hi):
                return nc.vector.tensor_tensor(dst, src, hi.bitcast(F32), ALU.subtract)

            def turn_to(hi_of_half, lo_of_half, number, width=P, ps=ps_turn):
                for h in range(2):
                    dve.wait_ge(turn_hi[h], number + 1)
                    rest(lo_of_half(h), ps[:, h, 0:4 * width].rearrange("p (k t) -> p k t", t=width),
                         hi_of_half(h)).then_inc(turn_lo[h], 1)

            def split_w(buf, visit, is_b=False):
                dve.wait_ge(w_hi_done[buf], visit + 1)
                if is_b:
                    rest(b_split_view(w_lo[buf]), b_raw_view(wraw[buf]),
                         b_split_view(w_hi[buf])).then_inc(w_lo_done[buf], 1)
                else:
                    rest(w_lo[buf][:], wraw[buf][:], w_hi[buf][:]).then_inc(w_lo_done[buf], 1)

            def turn_x(b, number):
                for h in range(2):
                    dve.wait_ge(turn_hi[h], number + 1)
                rest(xt_lo[b][:], xt_raw[b][:], xt_hi[b][:]).then_inc(xt_split[b], 1)

            split_w(0, 0, is_b=True)
            for v in range(V1_TURNS):
                turn_to(lambda h: vt1_hi[:, 4 * h:4 * h + 4, v * V1_ROWS:(v + 1) * V1_ROWS],
                        lambda h: vt1_lo[:, 4 * h:4 * h + 4, v * V1_ROWS:(v + 1) * V1_ROWS], v, V1_ROWS,
                        ps_turn_v[v % 2])
                if v == 1:
                    dve.wait_ge(small_hi, 1)
                    rest(vt1_lo[:, :, F1:HALF], ps_aw[:, 1, :].rearrange("p (k c) -> p k c", c=C),
                         vt1_hi[:, :, F1:HALF]).then_inc(small_lo, 1)

            def g_block(m, bank, visit):
                dve.wait_ge(g_hi_done[bank], visit + 1)
                at = (slice(None), bass.ds(m, 1), slice(0, F1))
                rest(g_lo[at].rearrange("p a f -> p (a f)"), ps_g[bank][:, 0:F1],
                     g_hi[at].rearrange("p a f -> p (a f)"))
                if isinstance(m, int) and m == 0:
                    lo, hi = gb[:, C:2 * C], gb[:, 0:C]
                else:
                    lo, hi = (aw[:, bass.ds(m - 1, 1), at:at + C].rearrange("p a c -> p (a c)") for at in (AWG, AW))
                rest(lo, ps_g[bank][:, F1:HALF], hi).then_inc(g_lo_done[bank], 1)

            split_w(1, 0)
            g_block(0, 0, 0)
            with dve.Fori(0, V2_TURNS // 2) as i:
                for s in range(2):
                    split_w(s, i + 1)
                    turn_to(lambda h: vt2_hi[:, 4 * h:4 * h + 4, bass.ts(2 * i + s, V2_ROWS)],
                            lambda h: vt2_lo[:, 4 * h:4 * h + 4, bass.ts(2 * i + s, V2_ROWS)],
                            TURN_V2 + 2 * i + s, V2_ROWS)
                    g_block(2 * i + s + 1, 1 - s, i + s)
            split_w(0, KD // 2)
            turn_to(lambda h: aw[:, 4 * h:4 * h + 4, 0:ER], lambda h: aw[:, 4 * h:4 * h + 4, LO_A:LO_WR], TURN_A)
            dve.wait_ge(small_hi, 2)
            rest(aw[:, :, LO_WR:2 * AWG], ps_aw[:, 0, 0:KD * E].rearrange("p (k e) -> p k e", e=E),
                 aw[:, :, ER:AW]).then_inc(small_lo, 1)
            g_block(KD - 1, 1, KD // 2 - 1)
            split_w(1, KD // 2, is_b=True)

            dve.wait_ge(const_ready, 5)
            dve.wait_ge(assign_landed, 32)
            nc.vector.memset(hit_sum[:], 0.0).then_inc(setup_step, 1)
            nc.vector.tensor_tensor(lang_bias[:], ids_raw[:].unsqueeze(2).broadcast_to([P, NB, E]),
                                    iota8[:].unsqueeze(1).broadcast_to([P, NB, E]),
                                    ALU.is_equal).then_inc(setup_step, 1)
            nc.vector.tensor_scalar(as_neg[:], as_raw[:], 0.0, float(C), ALU.is_lt, ALU.mult).then_inc(setup_step, 1)
            dve.wait_ge(setup_step, 3)
            nc.vector.tensor_scalar(lang_bias[:], lang_bias[:], LANG_BIAS, None, ALU.mult).then_inc(setup_step, 1)
            nc.vector.tensor_tensor(as_neg[:], as_raw[:], as_neg[:], ALU.add).then_inc(setup_step, 1)
            dve.wait_ge(setup_step, 5)
            nc.vector.tensor_scalar(as_neg[:], as_neg[:], 0.0, float(C - 1), ALU.max, ALU.min).then_inc(setup_step, 1)
            dve.wait_ge(setup_step, 6)
            nc.vector.tensor_scalar(onehot_a[:], as_neg[:], pidx[0:C, :], None, ALU.is_equal).then_inc(setup_step, 1)
            dve.wait_ge(setup_step, 7)
            g_block(KD, 0, KD // 2)

            def g_chunk(c, m):
                bank = BANK[c]
                dve.wait_ge(g_hi_done[bank], G_BASE[bank] + m + 1)
                at = (slice(None), bass.ds(m, 1), slice(F1 + c * CH, F1 + (c + 1) * CH))
                rest(g_lo[at].rearrange("p a f -> p (a f)"), ps_g[bank][:, 0:CH],
                     g_hi[at].rearrange("p a f -> p (a f)")).then_inc(g_lo_done[bank], 1)

            def route(n):
                base = ROUTER_STEPS * n

                def add_rest(c):
                    nc.vector.tensor_tensor(hg[:, c, :], ps_aw[:, c, 0:ER], aw_rest[:, c, 0:ER],
                                            ALU.add).then_inc(router, 1)

                dve.wait_ge(rest_taken, 2 * n + 2)
                nc.vector.tensor_tensor(rl[:], ps_aw[:, :, ER:AW], aw_rest[:, :, ER:AW], ALU.add).then_inc(router, 1)
                dve.wait_ge(router, base + 1)
                nc.vector.tensor_tensor(rl[:], rl[:], lang_bias[:, bass.ds(n, 1), :].broadcast_to([P, 2, E]),
                                        ALU.add).then_inc(router, 1)
                dve.wait_ge(router, base + 2)
                add_rest(0)
                for c in range(2):
                    nc.vector.max(m8[:, c, :], rl[:, c, :]).then_inc(router, 1)
                dve.wait_ge(router, base + 5)
                nc.vector.tensor_tensor(diff[:].unsqueeze(2), m8[:, :, 1:2], m8[:, :, 0:1],
                                        ALU.subtract).then_inc(router, 1)
                for c in range(2):
                    nc.vector.max_index(idx8[:, c, :], m8[:, c, :], rl[:, c, :]).then_inc(router, 1)
                add_rest(1)
                dve.wait_ge(router, base + 8)
                nc.vector.tensor_tensor(pick[:], iota8[:].unsqueeze(1).unsqueeze(1).broadcast_to([P, 2, 2, E]),
                                        idx8[:, :, 0:2].unsqueeze(3).broadcast_to([P, 2, 2, E]),
                                        ALU.is_equal).then_inc(router, 1)
                dve.wait_ge(e2_ready, n + 1)
                nc.vector.tensor_scalar(den[:], e2[:], 1.0, 1.0 / SCALING, ALU.add, ALU.mult).then_inc(router, 1)
                dve.wait_ge(router, base + 11)
                nc.vector.reciprocal(wts[:, :, 0], den[:]).then_inc(router, 1)
                dve.wait_ge(router, base + 12)
                nc.vector.tensor_tensor(wts[:, :, 1], wts[:, :, 0], e2[:], ALU.mult).then_inc(router, 1)
                dve.wait_ge(router, base + 13)
                nc.vector.tensor_tensor(pick[:], pick[:], wts[:].unsqueeze(3).broadcast_to([P, 2, 2, E]),
                                        ALU.mult).then_inc(router, 1)
                dve.wait_ge(router, base + 14)
                nc.vector.tensor_tensor(gates[:], pick[:, :, 0, :], pick[:, :, 1, :],
                                        ALU.add).then_inc(gates_ready, 1)
                dve.wait_ge(gates_ready, n + 1)
                nc.vector.tensor_tensor(hg[:].rearrange("p c (e r) -> p c e r", r=R),
                                        hg[:].rearrange("p c (e r) -> p c e r", r=R),
                                        gates[:].unsqueeze(3).broadcast_to([P, 2, E, R]),
                                        ALU.mult).then_inc(hg_ready, 1)

            def split_hgt(n):
                dve.wait_ge(hgt_hi_done, n + 1)
                rest(hgt_lo[:], ps_hgt, hgt_hi[:]).then_inc(hgt_lo_done, 1)
                nc.vector.tensor_copy(hgt_all[:, bass.ts(n, 2 * P)], ps_hgt).then_inc(hgt_stored, 1)

            def softmax_max(n):
                dve.wait_ge(logits_rest, n + 1)
                nc.vector.tensor_tensor(logits[:], ps_aw[:, :, AW:AWG], aw_rest[:, :, 0:C], ALU.add).then_inc(soft, 1)
                dve.wait_ge(soft, SOFT_STEPS * n + 1)
                nc.vector.tensor_reduce(mx[:], logits[:], AX_X, ALU.max).then_inc(soft, 1)
                dve.wait_ge(soft, SOFT_STEPS * n + 2)
                nc.vector.tensor_scalar(negb[:], mx[:], -1.0 / TEMPERATURE, None, ALU.mult).then_inc(soft, 1)

            def softmax_hits(n):
                dve.wait_ge(exp_done, 2 * n + 2)
                nc.vector.reciprocal(rsum[:], esum[:]).then_inc(soft, 1)
                dve.wait_ge(soft, SOFT_STEPS * n + 4)
                for c in range(2):
                    nc.vector.tensor_scalar(hits[:, c, :], ex[:, c, :], rsum[:, c:c + 1], THRESHOLD,
                                            ALU.mult, ALU.is_gt).then_inc(soft, 1)
                dve.wait_ge(soft, SOFT_STEPS * n + 6)
                nc.vector.tensor_reduce(qsel[:, bass.ts(n, 2)], hits[:], AX_X, ALU.max).then_inc(soft, 1)
                nc.vector.tensor_tensor(hit_sum[:], hit_sum[:], hits[:], ALU.add).then_inc(soft, 1)

            def second_sweep(n, buf, visit):
                first = isinstance(n, int) and n == 0
                if not first:
                    route(n - 1)
                    split_hgt(n - 1)
                turn_x(0, TURN_PAIR + 2 * n)
                if not first:
                    softmax_max(n - 1)
                turn_x(1, TURN_PAIR + 2 * n + 1)
                if not first:
                    softmax_hits(n - 1)
                split_w(buf, visit)
                for c in range(2):
                    g_chunk(c, n)

            second_sweep(0, 0, 5)
            with dve.Fori(0, NPAIR // 2 - 1) as i:
                second_sweep(2 * i + 1, 1, i + 5)
                second_sweep(2 * i + 2, 0, i + 6)
            second_sweep(NPAIR - 1, 1, 8)
            route(NPAIR - 1)

            def split_tile(b, visit, tile):
                dve.wait_ge(xt_hi_done[b], visit + 1)
                rest(xt_lo[b][:], xt_raw[b][:], xt_hi[b][:]).then_inc(xt_split[b], 1)
                dve.wait_ge(hx_hi_done, tile + 1)
                rest(hx_lo[b][:], hgt_all[:, bass.ts(tile, P)], hx_hi[b][:]).then_inc(hx_lo_done, 1)

            dve.wait_ge(hgt_stored, NPAIR - 1)
            split_tile(0, 0, 0)
            split_hgt(NPAIR - 1)
            softmax_max(NPAIR - 1)
            g_chunk(0, KD)
            softmax_hits(NPAIR - 1)
            dve.wait_ge(soft, SOFT_STEPS * NPAIR)
            nc.vector.tensor_copy(hit_b[:], hit_sum[:]).then_inc(hit_ready, 1)
            g_chunk(1, KD)
            dve.wait_ge(count_ready, 1)
            nc.vector.tensor_scalar(csel[:], ps_aw[0:C, 0, 0:P], 0.0, None, ALU.is_gt).then_inc(csel_ready, 1)
            split_tile(1, 0, 1)
            dve.wait_ge(hgt_stored, NPAIR)

            def finish(b, i, cols=slice(0, FO), part=0, ps=None):
                dve.wait_ge(main_ready[b], i + 1 + part)
                nc.vector.tensor_tensor(dense[:, cols], ps_out[:, 1 - b, cols] if ps is None else ps, bias_row[:, cols],
                                        ALU.add).then_inc(added[b], 1)
                dve.wait_ge(added[b], i + 1 + part)
                nc.vector.scalar_tensor_tensor(out=dense[:, cols], in0=dense[:, cols],
                                               scalar=qsel[:, bass.ds(2 * i + b, 1)], in1=mask_row[:, cols],
                                               op0=ALU.mult, op1=ALU.mult).then_inc(masked, 1)
                dve.wait_ge(masked, 2 * i + b + 1 + part)
                dve.wait_ge(x_landed[b], 16 * (NPAIR + 1 + i))
                nc.vector.tensor_tensor(xraw[b][:, cols], dense[:, cols], xraw[b][:, cols],
                                        ALU.add).then_inc(result_done[b], 1)

            dve.wait_ge(mask_done, 1)
            dve.wait_ge(bias_landed, 16)
            finish(0, 0)
            with dve.Fori(1, NPAIR) as i:
                split_tile(0, i, 2 * i)
                dve.wait_ge(result_done[0], i)
                finish(1, i - 1)
                split_tile(1, i, 2 * i + 1)
                dve.wait_ge(result_done[1], i)
                finish(0, i)
            dve.wait_ge(result_done[0], NPAIR)
            for c, cols in enumerate(LAST_PARTS):
                finish(1, NPAIR - 1, cols, c, ps_last[c])

        @block.tensor
        def _(pe):
            def turn(src_of_k, number, rows=P, ps=ps_turn, free=None):
                sems, count = free or (turn_lo, number)
                for h in range(2):
                    if not (isinstance(count, int) and count <= 0):
                        pe.wait_ge(sems[h], count)
                    for k in range(4):
                        last = nc.tensor.transpose(ps[:, h, k * rows:(k + 1) * rows], src_of_k(4 * h + k),
                                                   ident[0:rows, 0:rows])
                    last.then_inc(turned[h], 1)

            def turn_v(buf, rows, number, **where):
                turn(lambda j: vraw[buf][0:rows, j::KO], number, rows, **where)

            def turn_tile(b, visit, number):
                pe.wait_ge(x_landed[b], 16 * (visit + 1))
                free = (turn_lo, TURN_PAIR) if isinstance(number, int) and number == TURN_PAIR else (turn_hi, number)
                turn(lambda k: xraw[b][:, k * P:(k + 1) * P], number, free=free)

            def product(dst, left, right, j0=0, j1=KO):
                for j in range(j0, j1):
                    l_hi, l_lo = left(j)
                    r_hi, r_lo = right(j)
                    nc.tensor.matmul(dst, l_hi, r_hi, start=(j == 0), stop=False)
                    nc.tensor.matmul(dst, l_hi, r_lo, start=False, stop=False)
                    last = nc.tensor.matmul(dst, l_lo, r_hi, start=False, stop=(j == KO - 1))
                return last

            pe.wait_ge(const_ready, 2)
            for _ in range(WARM_UP):
                nc.tensor.transpose(ps_aw[:, 0, 0:P], ident[:], ident[:])

            def first_turn_v(v):
                pe.wait_ge(v_landed[v], 16)
                turn_v(v, V1_ROWS, v, ps=ps_turn_v[v % 2], free=(turn_lo, v - 1))

            first_turn_v(0)
            first_turn_v(1)
            pe.wait_ge(cent_landed, 16)
            for j in range(KO):
                last = nc.tensor.transpose(ps_aw[:, 1, j * C:(j + 1) * C], cent_raw[:, j::KO], ident[0:C, 0:C])
            last.then_inc(small_turned, 1)
            first_turn_v(2)

            def g_part(buf, bank, j0, j1, cols=slice(0, HALF)):
                return product(ps_g[bank][:, cols], lambda j: (w_hi[buf][:, j, :], w_lo[buf][:, j, :]),
                               lambda j: (vt1_hi[:, j, cols], vt1_lo[:, j, cols]), j0, j1)

            def first_sweep_step(buf, visit, turn_between=None):
                pe.wait_ge(w_lo_done[buf], visit + 1)
                if not (isinstance(visit, int) and visit == 0):
                    pe.wait_ge(g_lo_done[buf], visit)
                g_part(buf, buf, 0, 4)
                if turn_between is not None:
                    turn_between()
                g_part(buf, buf, 4, KO).then_inc(g_ready[buf], 1)

            def turn_a():
                pe.wait_ge(small_landed, 32)
                turn(lambda k: a_raw[:, k * P:(k + 1) * P], TURN_A)
                for k in range(KD):
                    last = nc.tensor.transpose(ps_aw[:, 0, k * E:(k + 1) * E], wr_raw[:, k * P:(k + 1) * P],
                                               ident[0:E, 0:E])
                last.then_inc(small_turned, 1)

            V_FIRST = V1_ROWS * V1_TURNS // 2
            pe.wait_ge(w_lo_done[0], 1)
            pe.wait_ge(turn_lo[0], V1_TURNS // 2)
            g_part(0, 0, 0, 4, slice(0, V_FIRST))
            first_turn_v(3)
            pe.wait_ge(turn_lo[1], V1_TURNS // 2)
            g_part(0, 0, 4, KO, slice(0, V_FIRST))
            pe.wait_ge(small_lo, 1)
            for h in range(2):
                pe.wait_ge(turn_lo[h], V1_TURNS)
                last = g_part(0, 0, 4 * h, 4 * h + 4, slice(V_FIRST, HALF))
            last.then_inc(g_ready[0], 1)

            def v2_turn(i, s):
                pe.wait_ge(v_landed[s], 16 * (i + 2))
                turn_v(s, V2_ROWS, TURN_V2 + 2 * i + s)

            pe.wait_ge(w_lo_done[1], 1)
            g_part(1, 1, 0, 4)
            v2_turn(0, 0)
            g_part(1, 1, 4, KO).then_inc(g_ready[1], 1)
            first_sweep_step(0, 1, lambda: v2_turn(0, 1))
            with pe.Fori(1, V2_TURNS // 2) as i:
                first_sweep_step(1, i, lambda: v2_turn(i, 0))
                first_sweep_step(0, i + 1, lambda: v2_turn(i, 1))
            first_sweep_step(1, KD // 2 - 1, turn_a)
            first_sweep_step(0, KD // 2)

            def g_chunk(buf, c, j0, j1):
                return product(ps_g[BANK[c]][:, 0:CH], lambda j: (w_hi[buf][:, j, :], w_lo[buf][:, j, :]),
                               lambda j: (vt2_hi[:, j, c * CH:(c + 1) * CH], vt2_lo[:, j, c * CH:(c + 1) * CH]),
                               j0, j1)

            def token_product(c, n):
                pe.wait_ge(xt_split[c], n + 1)
                for k in range(KD):
                    nc.tensor.matmul(ps_aw[:, c, 0:2 * AWG], xt_hi[c][:, k, :], aw[:, k, :], start=(k == 0),
                                     stop=(k == KD - 1))
                    last = nc.tensor.matmul(ps_aw[:, c, 0:AWG], xt_lo[c][:, k, :], aw[:, k, 0:AWG], start=False,
                                            stop=(k == KD - 1), skip_group_check=True)
                last.then_inc(aw_ready[c], 1)

            def turn_hg(n):
                pe.wait_ge(hg_ready, n + 1)
                if not (isinstance(n, int) and n == 0):
                    pe.wait_ge(hgt_stored, n)
                for c in range(2):
                    last = nc.tensor.transpose(ps_hgt[:, c * P:(c + 1) * P], hg[:, c, :], ident[:])
                last.then_inc(hgt_ready, 1)

            def lora_logits(n):
                pe.wait_ge(hgt_lo_done, n + 1)
                for c in range(2):
                    for left, width in ((hgt_hi, 2 * C), (hgt_lo, C)):
                        last = nc.tensor.matmul(ps_aw[:, c, AW:AW + width], left[:, c * P:(c + 1) * P],
                                                gb[:, 0:width], start=False, stop=True, skip_group_check=True)
                last.then_inc(logits_ready, 1)

            def second_sweep(n, buf, visit, prev=None, tokens=True):
                if tokens:
                    turn_tile(0, n, TURN_PAIR + 2 * n)
                pe.wait_ge(w_lo_done[buf], visit + 1)
                pe.wait_ge(g_lo_done[BANK[0]], G_BASE[BANK[0]] + n)
                g_chunk(buf, 0, 0, KO).then_inc(g_ready[BANK[0]], 1)
                pe.wait_ge(g_lo_done[BANK[1]], G_BASE[BANK[1]] + n)
                if not tokens:
                    g_chunk(buf, 1, 0, 2)
                    turn_hg(prev)
                    g_chunk(buf, 1, 2, 6)
                    lora_logits(prev)
                    g_chunk(buf, 1, 6, KO).then_inc(g_ready[BANK[1]], 1)
                    return
                if prev is not None:
                    turn_hg(prev)
                g_chunk(buf, 1, 0, 3)
                if prev is not None:
                    lora_logits(prev)
                turn_tile(1, n, TURN_PAIR + 2 * n + 1)
                g_chunk(buf, 1, 3, 4)
                if prev is not None:
                    pe.wait_ge(soft, SOFT_STEPS * prev + 1)
                token_product(0, n)
                g_chunk(buf, 1, 4, KO).then_inc(g_ready[BANK[1]], 1)
                token_product(1, n)

            pe.wait_ge(small_lo, 2)
            for h in range(2):
                pe.wait_ge(turn_lo[h], TURN_PAIR)
            second_sweep(0, 1, 4)
            second_sweep(1, 0, 5, 0)
            second_sweep(2, 1, 5, 1)
            with pe.Fori(1, NPAIR // 2 - 1) as i:
                second_sweep(2 * i + 1, 0, i + 5, 2 * i)
                second_sweep(2 * i + 2, 1, i + 5, 2 * i + 1)
            second_sweep(NPAIR - 1, 0, 8, NPAIR - 2)
            second_sweep(KD, 1, 8, NPAIR - 1, tokens=False)

            def hit_counts():
                pe.wait_ge(hit_ready, 1)
                for c in range(2):
                    last = nc.tensor.matmul(ps_aw[0:C, 0, 0:P], hit_b[:, c, :], ones_b[:], start=(c == 0), stop=(c == 1))
                last.then_inc(count_ready, 1)

            def column_mask():
                pe.wait_ge(csel_ready, 1)
                for c in range(2):
                    last = nc.tensor.matmul(ps_aw[:, c, :], csel[:], onehot_a[:, c * HALF:(c + 1) * HALF],
                                            start=True, stop=True)
                last.then_inc(mask_ready, 1)

            def main_tile(b, i, first=False, last_tile=False):
                pe.wait_ge(xt_split[b], NPAIR + 1 + i)
                if not first:
                    pe.wait_ge(added[b], i)
                whole = [(slice(c * HALF, (c + 1) * HALF), ps_out[:, 1 - b, c * HALF:(c + 1) * HALF]) for c in range(2)]
                for parts in [[part] for part in zip(LAST_PARTS, ps_last)] if last_tile else [whole]:
                    for k in range(KG):
                        l_hi = xt_hi[b][:, k, :] if k < KD else hx_hi[b][:]
                        l_lo = xt_lo[b][:, k, :] if k < KD else hx_lo[b][:]
                        r = k + 1 if k < KD else 0
                        if k == KD:
                            pe.wait_ge(hx_lo_done, 2 * i + b + 1)
                        if k == KD - 1 and first and b == 0:
                            for c in range(2):
                                pe.wait_ge(g_lo_done[c], G_BASE[c] + KG)
                        for left, g in ((l_hi, g_hi), (l_hi, g_lo), (l_lo, g_hi)):
                            for cols, ps in parts:
                                last = nc.tensor.matmul(ps, left, g[:, r, cols],
                                                        start=k == 0 and g is g_hi and left is l_hi,
                                                        stop=k == KD and left is l_lo)
                        if k == 3 and first and b == 0:
                            hit_counts()
                        if k == 5 and first and b == 0:
                            column_mask()
                    last.then_inc(main_ready[b], 1)

            pe.wait_ge(hgt_stored, NPAIR)
            main_tile(0, 0, first=True)
            main_tile(1, 0, first=True)
            with pe.Fori(1, NPAIR - 1) as i:
                for b in range(2):
                    main_tile(b, i)
            main_tile(0, NPAIR - 1)
            main_tile(1, NPAIR - 1, last_tile=True)


_INS = ["x", "itok_B_0_7", "L0_cond_W", "L0_cond_Wr", "L0_cond_A", "L0_cond_B",
        "L0_ffn_weight", "L0_ffn_bias", "L0_ffn_centroids", "L0_ffn_assignments"]


def kernel(**inputs):
    import numpy as np
    import concourse.bacc as bacc
    from concourse.bass_utils import run_bass_kernel_spmd

    nc = bacc.Bacc("TRN2", target_bir_lowering=False, num_devices=1)
    arrays, args = {}, []
    for name in _INS:
        a = np.ascontiguousarray(inputs[name])
        arrays[f"in_{name}"] = a
        args.append(nc.dram_tensor(f"in_{name}", a.shape, mybir.dt.from_np(a.dtype), kind="ExternalInput").ap())
    shape = inputs["x"].shape
    out = nc.dram_tensor("out_0", shape, F32, kind="ExternalOutput").ap()
    adaln_ffn_kernel(nc, *args, out)
    r = run_bass_kernel_spmd(nc, [arrays], core_ids=[0])
    return r.results[0]["out_0"]
```
